# Optimizing a Trainium2 kernel written in Bass

```python
import numpy as np
import jax
import jax.numpy as jnp

def _softmax(x, axis=-1):
    return jax.nn.softmax(x, axis=axis)

def _gelu(x):
    return jax.nn.gelu(x, approximate=True)

def _silu(x):
    return jax.nn.silu(x)

def _sigmoid(x):
    return jax.nn.sigmoid(x)

def _layernorm(x, axis=-1, eps=1e-05):
    m = jnp.mean(x, axis=axis, keepdims=True)
    v = jnp.var(x, axis=axis, keepdims=True)
    return (x - m) / jnp.sqrt(v + eps)

def _scatter_add(tgt, idx, src, axis=0):
    return tgt.at[idx].add(src)

def _segment_sum(src, seg, n):
    return jax.ops.segment_sum(src, seg, n)
kernel_name = 'mk_flamingo_gated_d1_seqx_r8_256cd6'

def setup_inputs(seed: int=0):
    np.random.seed(seed)
    _w = jnp.asarray

    def _rec_inputs():
        import jax
        import jax.numpy as jnp
        _rk = jax.random.key(seed)
        x = -0.0002928 + 1 * jax.random.normal(jax.random.fold_in(_rk, 1), (8, 256, 128), jnp.float32)
        _lenS = 256 - jax.random.randint(jax.random.fold_in(_rk, 7), (8,), 0, max(1, 256 // 4) + 1, jnp.int32)
        _lenS2 = 256 - jax.random.randint(jax.random.fold_in(_rk, 8), (8,), 0, max(1, 256 // 4) + 1, jnp.int32)
        _ctx_512P = jax.random.normal(jax.random.fold_in(_rk, 11), (8, 16, 64), jnp.float32)
        _ctx_512c = jax.random.dirichlet(jax.random.fold_in(_rk, 511), 0.3 * jnp.ones((16,), jnp.float32), (8, 256))
        _ctx_512t = jnp.einsum('bsk,bkd->bsd', _ctx_512c, _ctx_512P)
        _ctx_512t = _ctx_512t * jax.lax.rsqrt(jnp.mean(jnp.square(_ctx_512t)) + 1e-12) * 0.953939
        ctx_512 = 0.00222621 + 0.99962 * (_ctx_512t + 0.3 * jax.random.normal(jax.random.fold_in(_rk, 611), (8, 256, 64), jnp.float32))
        _g = jax.random.normal(jax.random.fold_in(_rk, 9001), (2, 1), jnp.float32)
        _g = jnp.sign(_g) * jnp.maximum(jnp.abs(_g), 1.0) + (_g == 0) * 1.0
        g_xattn = _g[0]
        g_ffn = _g[1]
        return (x, ctx_512, g_xattn, g_ffn)
    x, ctx_512, g_xattn, g_ffn = _rec_inputs()

    def _L0_xattn_setup():
        import jax, jax.numpy as jnp
        import numpy as np
        B, T, TC, C, CC, H = (2, 256, 64, 128, 64, 16)
        D = C // H

        def _heads(t):
            b, l, _ = t.shape
            return t.reshape(b, l, H, D).transpose(0, 2, 1, 3)
        key = jax.random.key(seed)
        ks = jax.random.split(key, 18)
        w = lambda k, i, o: jax.random.normal(k, (i, o), jnp.float32) / np.sqrt(i).astype(np.float32)
        return {'x': jax.random.normal(ks[0], (B, T, C), jnp.float32), 'cross_input': jax.random.normal(ks[1], (B, TC, CC), jnp.float32), 'Wk': w(ks[2], C, C), 'bk': jnp.zeros((C,), jnp.float32), 'Wq': w(ks[3], C, C), 'bq': jnp.zeros((C,), jnp.float32), 'Wv': w(ks[4], C, C), 'bv': jnp.zeros((C,), jnp.float32), 'Wck': w(ks[5], CC, C), 'bck': jnp.zeros((C,), jnp.float32), 'Wcq': w(ks[6], C, C), 'bcq': jnp.zeros((C,), jnp.float32), 'Wcv': w(ks[7], CC, C), 'bcv': jnp.zeros((C,), jnp.float32), 'Wp': w(ks[8], C, C), 'bp': jnp.zeros((C,), jnp.float32)}
    _L0_xattn_all = _L0_xattn_setup()
    _L0_xattn_in = {k: v for k, v in _L0_xattn_all.items() if k in ('Wk', 'bk', 'Wq', 'bq', 'Wv', 'bv', 'Wck', 'bck', 'Wcq', 'bcq', 'Wcv', 'bcv', 'Wp', 'bp')}
    del _L0_xattn_all

    def _L0_ffn_setup():
        import jax, jax.numpy as jnp
        import numpy as np
        HIDDEN = 128
        INTER = 256
        NUM_EXPERTS = 8
        TOPK = 2
        STD = 0.02
        key = jax.random.key(seed)
        k1, k2, k3, k4 = jax.random.split(key, 4)
        return {'hidden_states': jax.random.normal(k1, (1, 256, HIDDEN), dtype=jnp.float32), 'w1': jax.random.normal(k2, (NUM_EXPERTS, 2 * INTER, HIDDEN), dtype=jnp.float32) * STD, 'w2': jax.random.normal(k3, (NUM_EXPERTS, HIDDEN, INTER), dtype=jnp.float32) * STD, 'router_w': jax.random.normal(k4, (NUM_EXPERTS, HIDDEN), dtype=jnp.float32) * STD}
    _L0_ffn_all = _L0_ffn_setup()
    _L0_ffn_in = {k: v for k, v in _L0_ffn_all.items() if k in ('w1', 'w2', 'router_w')}
    del _L0_ffn_all
    return {'x': x, 'ctx_512': ctx_512, 'g_xattn': g_xattn, 'g_ffn': g_ffn, 'L0_xattn_Wk': _L0_xattn_in['Wk'], 'L0_xattn_bk': _L0_xattn_in['bk'], 'L0_xattn_Wq': _L0_xattn_in['Wq'], 'L0_xattn_bq': _L0_xattn_in['bq'], 'L0_xattn_Wv': _L0_xattn_in['Wv'], 'L0_xattn_bv': _L0_xattn_in['bv'], 'L0_xattn_Wck': _L0_xattn_in['Wck'], 'L0_xattn_bck': _L0_xattn_in['bck'], 'L0_xattn_Wcq': _L0_xattn_in['Wcq'], 'L0_xattn_bcq': _L0_xattn_in['bcq'], 'L0_xattn_Wcv': _L0_xattn_in['Wcv'], 'L0_xattn_bcv': _L0_xattn_in['bcv'], 'L0_xattn_Wp': _L0_xattn_in['Wp'], 'L0_xattn_bp': _L0_xattn_in['bp'], 'L0_ffn_w1': _L0_ffn_in['w1'], 'L0_ffn_w2': _L0_ffn_in['w2'], 'L0_ffn_router_w': _L0_ffn_in['router_w']}

def reference(x, ctx_512, g_xattn, g_ffn, L0_xattn_Wk, L0_xattn_bk, L0_xattn_Wq, L0_xattn_bq, L0_xattn_Wv, L0_xattn_bv, L0_xattn_Wck, L0_xattn_bck, L0_xattn_Wcq, L0_xattn_bcq, L0_xattn_Wcv, L0_xattn_bcv, L0_xattn_Wp, L0_xattn_bp, L0_ffn_w1, L0_ffn_w2, L0_ffn_router_w):
    import jax
    import jax.numpy as jnp

    def _L0_xattn_ref(x, cross_input, Wk, bk, Wq, bq, Wv, bv, Wck, bck, Wcq, bcq, Wcv, bcv, Wp, bp):
        import jax, jax.numpy as jnp
        import numpy as np
        B, T, TC, C, CC, H = (2, 256, 64, 128, 64, 16)
        D = C // H

        def _heads(t):
            b, l, _ = t.shape
            return t.reshape(b, l, H, D).transpose(0, 2, 1, 3)
        scale = np.float32(1.0 / np.sqrt(D))
        q = _heads(x @ Wq + bq)
        k = _heads(x @ Wk + bk)
        v = _heads(x @ Wv + bv)
        att = jnp.einsum('bhqd,bhkd->bhqk', q, k) * scale
        causal = jnp.tril(jnp.ones((T, T), bool))
        att = jnp.where(causal[None, None], att, -jnp.inf)
        y = jnp.einsum('bhqk,bhkd->bhqd', jax.nn.softmax(att, axis=-1), v)
        qc = _heads(x @ Wcq + bcq)
        kc = _heads(cross_input @ Wck + bck)
        vc = _heads(cross_input @ Wcv + bcv)
        attc = jnp.einsum('bhqd,bhkd->bhqk', qc, kc) * scale
        y = y + jnp.einsum('bhqk,bhkd->bhqd', jax.nn.softmax(attc, axis=-1), vc)
        y = y.transpose(0, 2, 1, 3).reshape(x.shape[0], T, C)
        return y @ Wp + bp

    def _L0_ffn_ref(hidden_states, w1, w2, router_w):
        import jax, jax.numpy as jnp
        import numpy as np
        HIDDEN = 128
        INTER = 256
        NUM_EXPERTS = 8
        TOPK = 2
        STD = 0.02
        orig_shape = hidden_states.shape
        dtype = hidden_states.dtype
        x = hidden_states.reshape(-1, orig_shape[-1])
        E = w1.shape[0]
        gating = x @ router_w.T
        probs = jax.nn.softmax(gating.astype(jnp.float32), axis=-1)
        topk_w, sel = jax.lax.top_k(probs, TOPK)
        topk_w = topk_w.astype(dtype)
        combine = (jax.nn.one_hot(sel, E, dtype=dtype) * topk_w[..., None]).sum(axis=1)
        h = jnp.einsum('td,eid->tei', x, w1)
        gate = jax.nn.silu(h[..., :INTER])
        y = h[..., INTER:] * gate
        out = jnp.einsum('tei,ehi,te->th', y, w2, combine)
        return out.reshape(orig_shape)
    x = x + jnp.tanh(g_xattn[0]) * _L0_xattn_ref(_layernorm(x, axis=-1), ctx_512, L0_xattn_Wk, L0_xattn_bk, L0_xattn_Wq, L0_xattn_bq, L0_xattn_Wv, L0_xattn_bv, L0_xattn_Wck, L0_xattn_bck, L0_xattn_Wcq, L0_xattn_bcq, L0_xattn_Wcv, L0_xattn_bcv, L0_xattn_Wp, L0_xattn_bp)
    x = x + jnp.tanh(g_ffn[0]) * _L0_ffn_ref(_layernorm(x, axis=-1), L0_ffn_w1, L0_ffn_w2, L0_ffn_router_w)
    return x

_drawn_inputs = setup_inputs


def setup_inputs(seed=0):
    import zlib

    import numpy as np

    out = dict(_drawn_inputs(seed))
    spreads = {'L0_xattn_bk': (0.0, 0.8),
     'L0_xattn_bq': (0.0, 0.563),
     'L0_xattn_bv': (0.0, 0.1),
     'L0_xattn_bck': (0.0, 0.8),
     'L0_xattn_bcq': (0.0, 0.483),
     'L0_xattn_bcv': (0.0, 0.1),
     'L0_xattn_bp': (0.0, 0.1)}
    factors = {'L0_ffn_w1': 8.0, 'L0_ffn_w2': 8.0, 'L0_ffn_router_w': 8.0}
    for name, (base, spread) in spreads.items():
        noise = np.random.default_rng([zlib.crc32(name.encode()), seed]).standard_normal(out[name].shape)
        drawn = base * np.exp(spread * noise) if base else spread * noise
        out[name] = jnp.asarray(drawn.astype(out[name].dtype))
    for name, factor in factors.items():
        out[name] = (out[name] * factor).astype(out[name].dtype)
    return out
```

```python
from contextlib import ExitStack

import concourse.bass as bass
from concourse import mybir

F32 = mybir.dt.float32
F32R = mybir.dt.float32r
BF16 = mybir.dt.bfloat16
ALU = mybir.AluOpType
ACT = mybir.ActivationFunctionType
AX_X = mybir.AxisListType.X

P = 128
NB, T, C = 8, 256, 128
CC = 64
H, D = 16, 8
QT = T // P
NTILE = NB * QT
STEPS = 8
GH = 4
QUAD = P // GH
SCALE = float(D) ** -0.5
MASKED = -1e30
EPS = 1e-5
PRODUCTS = [(0, 0), (0, 1), (0, 2), (1, 0), (1, 1), (2, 0)]
HEAD_ROWS = len(PRODUCTS) * D
ROWS = 2 * HEAD_ROWS
MROWS = ROWS + 3
Q, K, KC, QC = range(4)
NE, INTER, TOPK = 8, 256, 2
CHUNK = 512
NCHUNK = NB * T // CHUNK
CT = CHUNK // P
IT = INTER // P


def gated_attention_experts(nc, x, ctx_in, gates, wqk, wck, bqk, wv, wcv, wp, bvp, w1t, w2t, rwt, out):
    with ExitStack() as es, ExitStack() as attention:
        def kept(name, shape, dt=F32):
            return es.enter_context(nc.sbuf_tensor(name, shape, dt))

        def sb(name, shape, dt=F32):
            return attention.enter_context(nc.sbuf_tensor(name, shape, dt))

        def sem(name):
            return es.enter_context(nc.semaphore(name))

        x_all = kept("x_all", [P, NTILE, C])
        tgate = kept("tgate", [P, 2])
        ident = kept("ident", [P, P])
        identb = kept("identb", [P, P], BF16)
        minus_half = kept("minus_half", [P, CT])
        w1_hi = kept("w1_hi", [P, NE, 2 * INTER], F32R)
        w1_lo = kept("w1_lo", [P, NE, 2 * INTER], F32R)
        w2_hi = kept("w2_hi", [P, NE, IT, C], F32R)
        w2_lo = kept("w2_lo", [P, NE, IT, C], F32R)
        rw_sb = kept("rw_sb", [P, NE])
        ctx_sb = sb("ctx_sb", [P, 2, QT, CC])
        wqk_sb = sb("wqk_sb", [P, 3, C])
        wck_sb = sb("wck_sb", [CC, C])
        bqk_sb = sb("bqk_sb", [P, 4])
        wv_sb = sb("wv_sb", [P, C])
        wcv_sb = sb("wcv_sb", [CC, C])
        wp_sb = sb("wp_sb", [P, C])
        bvp_sb = sb("bvp_sb", [P, 3, C])
        gate_sb = sb("gate_sb", [P, 2])
        mask_qk = sb("mask_qk", [P, P], BF16)
        mask_kq = sb("mask_kq", [P, P], BF16)
        qstack = sb("qstack", [MROWS, 2, 2, H, T], BF16)
        kstack = sb("kstack", [MROWS, 2, 2, H // 2, T], BF16)
        vext = sb("vext", [P, 2, 2, QT, H, QUAD])
        xn = sb("xn", [P, QT, C])
        xnT = sb("xnT", [P, T])
        ctxT = sb("ctxT", [CC, T])
        stats = sb("stats", [P, QT, 6])
        meanvar = sb("meanvar", [P, QT, 2])
        vareps = sb("vareps", [P, QT])
        rstd = sb("rstd", [P, QT])
        part = sb("part", [P, 4, 3, T], BF16)
        resid = sb("resid", [P, 4, T])
        rowmax = sb("rowmax", [P, 4, QT, GH])
        negmax = sb("negmax", [P, QT, GH])
        negres = sb("negres", [P, QT, GH])
        mparts = sb("mparts", [P, 2, QT, 3, GH], BF16)
        mrows = sb("mrows", [3 * GH, 2, T], BF16)
        probs = sb("probs", [P, 2 * GH, 2 * T])
        o_sb = sb("o_sb", [P, 2, 2 * T])
        rden = sb("rden", [P, 2, QT, GH])
        ynorm = sb("ynorm", [P, 2, QT, GH, D])
        y_sb = sb("y_sb", [P, QT, C])
        yT = sb("yT", [P, T])
        proj_b = sb("proj_b", [P, QT, C])
        w1_sb = sb("w1_sb", [P, NE, 2 * INTER])
        w2_sb = sb("w2_sb", [P, NE, IT, C])

        psum = es.enter_context(nc.psum_tensor("psum", [P, 8, 512], F32))
        bank_a = [psum[:, 0, :], psum[:, 1, :]]
        bank_b = [psum[:, 2, :], psum[:, 3, :]]
        bank_o = psum[:, 4, :]
        bank_t = psum[:, 5, :]
        bank_f = psum[:, 6, :]
        bank_m = psum[:, 7, :].bitcast(BF16)

        w_in, x_in, moe_in = sem("w_in"), sem("x_in"), sem("moe_in")
        ctx_loaded = [sem("ctx_loaded0"), sem("ctx_loaded1")]
        const_pool, const_dve = sem("const_pool"), sem("const_dve")
        gate_done = sem("gate_done")
        ln_step = sem("ln_step")
        rooted = sem("rooted")
        front_filled = sem("front_filled")
        front_act = sem("front_act")
        front_dve = sem("front_dve")
        low_done = sem("low_done")
        stacked = [sem(f"stacked{n}") for n in range(4)]
        scored = sem("scored")
        maxed = sem("maxed")
        msplit = sem("msplit")
        m_turned = sem("m_turned")
        m_copied = sem("m_copied")
        m_placed = [sem("m_placed0"), sem("m_placed1")]
        shifted = sem("shifted")
        exped = sem("exped")
        weighed = sem("weighed")
        o_copied = sem("o_copied")
        o_turned = sem("o_turned")
        normed = sem("normed")
        y_turned, y_copied, projected = sem("y_turned"), sem("y_copied"), sem("projected")
        x1_step = sem("x1_step")
        w_hi_done, w_lo_done = sem("w_hi_done"), sem("w_lo_done")

        def group(s):
            return s % 2, GH * (s // 2)

        LEAD, TURN = 3, 2

        def pe_scores(pe, b, par, s):
            attn, h0 = group(s)
            for j in range(GH):
                if s == attn and j == 0:
                    pe.wait_ge(stacked[QC if attn else Q], 16 * 2 * len(PRODUCTS) * (b + 1))
                    pe.wait_ge(stacked[KC if attn else K], 16 * 2 * len(PRODUCTS) * (b + 1))
                yield
                u = (b * STEPS + s) * GH + j
                if not (isinstance(u, int) and u < 2):
                    pe.wait_ge(maxed, u - 1)
                q = qstack[0:ROWS, par, attn, h0 + j, :]
                k = kstack[0:ROWS, par, attn, (h0 + j) % (H // 2), :]
                a = bank_a[j % 2]
                if attn == 0:
                    nc.tensor.matmul(a[:, 0:P], q[:, 0:P], k[:, 0:P], start=True, stop=False)
                    nc.tensor.matmul(a[:, 0:P], identb[:, :], mask_qk[:, :], start=False, stop=True)
                    nc.tensor.matmul(a[:, P:P + T], q[:, P:T], k[:, :], start=True, stop=True)
                    mm = nc.tensor.matmul(a[:, T:T + P], identb[:, :], mask_qk[:, :], start=False, stop=True,
                                          skip_group_check=True)
                else:
                    nc.tensor.matmul(a[:, 0:T], q[:, 0:P], k[:, :], start=True, stop=True)
                    mm = nc.tensor.matmul(a[:, T:2 * T], q[:, P:T], k[:, :], start=True, stop=True)
                mm.then_inc(scored, 1)
                yield

        def pe_shifted(pe, b, par, s):
            attn, h0 = group(s)
            for j in range(GH):
                if j == 0:
                    pe.wait_ge(m_placed[s % 2], 16 * (b * 4 + s // 2 + 1))
                u = (b * STEPS + s) * GH + j
                if not (isinstance(u, int) and u < 2):
                    pe.wait_ge(exped, u - 1)
                q = qstack[0:MROWS, par, attn, h0 + j, :]
                k = kstack[0:MROWS, par, attn, (h0 + j) % (H // 2), :]
                s_b = bank_b[j % 2]
                if attn == 0:
                    nc.tensor.matmul(s_b[:, 0:T], k[:, 0:P], q[:, :], start=True, stop=True)
                    nc.tensor.matmul(s_b[:, 0:P], identb[:, :], mask_kq[:, :], start=False, stop=True,
                                     skip_group_check=True)
                    nc.tensor.matmul(s_b[:, T:T + P], k[:, P:T], q[:, P:T], start=True, stop=False)
                    mm = nc.tensor.matmul(s_b[:, T:T + P], identb[:, :], mask_kq[:, :], start=False, stop=True)
                else:
                    nc.tensor.matmul(s_b[:, 0:T], k[:, 0:P], q[:, :], start=True, stop=True)
                    mm = nc.tensor.matmul(s_b[:, T:2 * T], k[:, P:T], q[:, :], start=True, stop=True)
                mm.then_inc(shifted, 1)
                yield

        def pe_weigh(pe, b, par, s):
            attn, h0 = group(s)
            g = b * STEPS + s
            pe.wait_ge(exped, GH * (g + 1))
            if s == 0:
                pe.wait_ge(front_dve, 10 * (b + 1))
            if attn == 0 and not (isinstance(g, int) and g == 0):
                pe.wait_ge(o_copied, b * 4 + s // 2)
            for key_tile in range(2):
                for j in range(GH):
                    first = key_tile == 0
                    skip = P if attn == 0 and not first else 0
                    pr = probs[:, GH * (s % 2) + j, T * key_tile:T * (key_tile + 1) - skip]
                    mm = nc.tensor.matmul(bank_o[QUAD * j:QUAD * (j + 1), T * attn + skip:T * (attn + 1)],
                                          vext[:, par, attn, key_tile, h0 + j, :], pr, start=first,
                                          stop=True, skip_group_check=True)
            mm.then_inc(weighed, 1)

        def pe_turn_max(pe, b, s):
            g = b * STEPS + s
            pe.wait_ge(msplit, 5 * (g + 1))
            if not (isinstance(g, int) and g == 0):
                pe.wait_ge(m_copied, g)
            for t in range(QT):
                mm = nc.tensor.transpose(bank_m[0:3 * GH, P * t:P * (t + 1)],
                                         mparts[:, s % 2, t, :, :].rearrange("p c h -> p (c h)"), identb[:, :])
            mm.then_inc(m_turned, 1)

        def pe_turn_out(pe, b, r):
            pair = b * 4 + r
            pe.wait_ge(o_copied, pair + 1)
            if r == 0 and not (isinstance(b, int) and b == 0):
                pe.wait_ge(x1_step, 2 * b)
            if r > 0:
                pe.wait_ge(normed, 3 * pair)
            for n in range(4):
                mm = nc.tensor.transpose(bank_t[:, P * n:P * (n + 1)], o_sb[:, r % 2, P * n:P * (n + 1)],
                                         ident[:, :])
            mm.then_inc(o_turned, 1)

        def pe_turn_y(pe, b):
            pe.wait_ge(normed, 3 * 4 * (b + 1))
            for t in range(QT):
                mm = nc.tensor.transpose(bank_t[:, P * t:P * (t + 1)], y_sb[:, t, :], ident[:, :])
            mm.then_inc(y_turned, 1)

        def pe_project(pe, b):
            pe.wait_ge(y_copied, b + 1)
            for t in range(QT):
                mm = nc.tensor.matmul(bank_t[:, P * t:P * (t + 1)], yT[:, P * t:P * (t + 1)], wp_sb[:, :],
                                      start=True, stop=True)
            mm.then_inc(projected, 1)

        def pe_front(pe, b, par, item):
            if item == 0:
                if not (isinstance(b, int) and b == 0):
                    pe.wait_ge(front_dve, 10 * b)
                pe.wait_ge(ln_step, 7 * (b + 1))
                for t in range(QT):
                    mm = nc.tensor.transpose(bank_f[:, P * t:P * (t + 1)], xn[:, t, :], ident[:, :])
            elif item in (1, 2, 5):
                if item == 1:
                    pe.wait_ge(front_act, 6 * b + 1)
                elif item == 2:
                    pe.wait_ge(front_dve, 10 * b + 1)
                else:
                    pe.wait_ge(front_dve, 10 * b + 5)
                mm = nc.tensor.matmul(bank_f[:, 0:T], wqk_sb[:, {1: 0, 2: 1, 5: 2}[item], :], xnT[:, :],
                                      start=True, stop=True)
            elif item == 3:
                pe.wait_ge(front_dve, 10 * b + 3)
                if isinstance(b, int):
                    pe.wait_ge(ctx_loaded[par], 16 * (b // 2 + 1))
                else:
                    pe.wait_ge(ctx_loaded[par], 8 * (b - par) + 16)
                pe.nop(nofuse=True)
                for t in range(QT):
                    mm = nc.tensor.transpose(bank_f[0:CC, P * t:P * (t + 1)], ctx_sb[:, par, t, :], ident[:, :])
            elif item == 4:
                pe.wait_ge(front_act, 6 * b + 4)
                mm = nc.tensor.matmul(bank_f[:, 0:T], wck_sb[:, :], ctxT[:, :], start=True, stop=True)
            else:
                pe.wait_ge(front_dve, 10 * b + (7 if item == 6 else 9))
                src, w = (xnT, wv_sb) if item == 6 else (ctxT, wcv_sb)
                for t in range(QT):
                    mm = nc.tensor.matmul(bank_f[:, P * t:P * (t + 1)], src[:, P * t:P * (t + 1)], w[:, :],
                                          start=True, stop=True)
            mm.then_inc(front_filled, 1)

        def later(b, par, s, by):
            return (b, par, s + by) if s + by < STEPS else (b + 1, 1 - par, s + by - STEPS)

        def pe_batch(pe, b, par, first=False, last=False):
            for s in range(STEPS):
                ahead = None if last and s + LEAD >= STEPS else pe_scores(pe, *later(b, par, s, LEAD))
                shift = pe_shifted(pe, b, par, s)
                for j in range(GH):
                    next(shift)
                    if ahead:
                        next(ahead)
                        next(ahead)
                    if j == 0:
                        if s == 2 and not first:
                            pe_project(pe, b - 1)
                        if s > 0:
                            pe_weigh(pe, b, par, s - 1)
                        elif not first:
                            pe_weigh(pe, b - 1, 1 - par, STEPS - 1)
                    if j == 1 and not last and 1 <= s <= 4:
                        pe_front(pe, b + 1, 1 - par, 2 * s - 2)
                    if j == 2:
                        if not (last and s + TURN >= STEPS):
                            tb, _, ts = later(b, par, s, TURN)
                            pe_turn_max(pe, tb, ts)
                        if s == 1 and not first:
                            pe_turn_y(pe, b - 1)
                        if s % 2 == 0 and s > 0:
                            pe_turn_out(pe, b, s // 2 - 1)
                        elif s == 0 and not first:
                            pe_turn_out(pe, b - 1, 3)
                    if j == 3 and not last and 1 <= s <= 4:
                        pe_front(pe, b + 1, 1 - par, 2 * s - 1)

        def dve_norm_x(dve, b):
            if not (isinstance(b, int) and b == 0):
                dve.wait_ge(front_filled, 8 * (b - 1) + 1)
            for t in range(QT):
                nc.vector.bn_stats(stats[:, t, :], x_all[:, QT * b + t, :]).then_inc(ln_step, 1)
            for t in range(QT):
                dve.wait_ge(ln_step, 7 * b + 1 + t)
                dve.nop(nofuse=True)
                nc.vector.bn_aggr(meanvar[:, t, :], stats[:, t, :]).then_inc(ln_step, 1)
            dve.wait_ge(ln_step, 7 * b + 4)
            nc.vector.tensor_scalar(vareps[:, :], meanvar[:, :, 1], EPS, None, ALU.add).then_inc(ln_step, 1)
            dve.wait_ge(rooted, b + 1)
            for t in range(QT):
                nc.vector.tensor_scalar(xn[:, t, :], x_all[:, QT * b + t, :], meanvar[:, t, 0:1], rstd[:, t:t + 1],
                                        ALU.subtract, ALU.mult).then_inc(ln_step, 1)

        def dve_max(dve, b, s):
            attn, _ = group(s)
            for j in range(GH):
                g = b * STEPS + s
                dve.wait_ge(scored, GH * g + j + 1)
                if j == 0 and not (isinstance(g, int) and g < 4):
                    dve.wait_ge(msplit, 5 * (g - 3))
                a = bank_a[j % 2]
                if attn == 0:
                    nc.vector.tensor_reduce(rowmax[:, s % 4, 0, j:j + 1], a[:, 0:P], AX_X, ALU.max)
                    op = nc.vector.tensor_reduce(rowmax[:, s % 4, 1, j:j + 1], a[:, P:P + T], AX_X, ALU.max)
                else:
                    op = nc.vector.tensor_reduce(rowmax[:, s % 4, :, j], a.rearrange("p (t k) -> p t k", t=QT),
                                                 AX_X, ALU.max)
                op.then_inc(maxed, 1)
                yield

        def dve_front(dve, b, par, item):
            if item in (1, 2, 4, 5):
                n = {1: Q, 2: K, 4: KC, 5: QC}[item]
                dve.wait_ge(front_act, 6 * b + {1: 2, 2: 3, 4: 5, 5: 6}[item])
                step = 10 * b + {1: 0, 2: 2, 4: 4, 5: 6}[item]
                nc.vector.scalar_tensor_tensor(out=resid[:, n, :], in0=bank_f[:, 0:T], scalar=bqk_sb[:, n:n + 1],
                                               in1=part[:, n, 0, :], op0=ALU.add, op1=ALU.subtract)\
                    .then_inc(front_dve, 1)
                dve.wait_ge(front_dve, step + 1)
                nc.vector.tensor_copy(part[:, n, 1, :], resid[:, n, :]).then_inc(front_dve, 1)
            elif item in (6, 7):
                dve.wait_ge(front_filled, 8 * b + item + 1)
                if not (isinstance(b, int) and b < 2):
                    dve.wait_ge(weighed, STEPS * (b - 1))
                attn = item - 6
                nc.vector.tensor_tensor(
                    vext[:, par, attn, :, :, 0:D],
                    bank_f[:, 0:T].rearrange("p (t h d) -> p t h d", t=QT, d=D),
                    bvp_sb[:, attn, :].rearrange("p (h d) -> p h d", d=D).unsqueeze(1).to_broadcast([P, QT, H, D]),
                    ALU.add).then_inc(front_dve, 1)

        def dve_norm_out(dve, b, r):
            pair = b * 4 + r
            dve.wait_ge(o_turned, pair + 1)
            t = bank_t.rearrange("p (a t j f) -> p a t j f", a=2, t=QT, j=GH)
            nc.vector.reciprocal(rden[:, :, :, :], t[:, :, :, :, D]).then_inc(normed, 1)
            dve.wait_ge(normed, 3 * pair + 1)
            for attn in range(2):
                op = nc.vector.tensor_tensor(ynorm[:, attn], t[:, attn, :, :, 0:D],
                                             rden[:, attn].unsqueeze(3).to_broadcast([P, QT, GH, D]), ALU.mult)
            op.then_inc(normed, 1)
            dve.wait_ge(normed, 3 * pair + 2)
            if r == 0 and not (isinstance(b, int) and b == 0):
                dve.wait_ge(y_turned, b)
            nc.vector.tensor_tensor(y_sb[:, :, QUAD * r:QUAD * (r + 1)].rearrange("p t (j d) -> p t j d", d=D),
                                    ynorm[:, 0], ynorm[:, 1], ALU.add).then_inc(normed, 1)

        def dve_residual(dve, b):
            dve.wait_ge(projected, b + 1)
            nc.vector.tensor_tensor(proj_b[:, :, :], bank_t[:, 0:T].rearrange("p (t c) -> p t c", t=QT),
                                    bvp_sb[:, 2, :].unsqueeze(1).to_broadcast([P, QT, C]), ALU.add)\
                .then_inc(x1_step, 1)
            dve.wait_ge(x1_step, 2 * b + 1)
            for t in range(QT):
                op = nc.vector.scalar_tensor_tensor(out=x_all[:, QT * b + t, :], in0=proj_b[:, t, :],
                                                    scalar=tgate[:, 0:1], in1=x_all[:, QT * b + t, :],
                                                    op0=ALU.mult, op1=ALU.add)
            op.then_inc(x1_step, 1)

        def dve_batch(dve, b, par, first=False, last=False):
            for s in range(STEPS):
                if s == 0 and not last:
                    dve_norm_x(dve, b + 1)
                ahead = None
                if not (last and s + LEAD >= STEPS):
                    ab, _, a_s = later(b, par, s, LEAD)
                    ahead = dve_max(dve, ab, a_s)
                for j in range(GH):
                    if ahead:
                        next(ahead)
                    if j == 1 and not last and 1 <= s <= 4:
                        dve_front(dve, b + 1, 1 - par, 2 * s - 2)
                    if j == 0 and s == 2 and not first:
                        dve_residual(dve, b - 1)
                    if j == 2:
                        if s % 2 == 0 and s > 0:
                            dve_norm_out(dve, b, s // 2 - 1)
                        elif s == 0 and not first:
                            dve_norm_out(dve, b - 1, 3)
                    if j == 3 and not last and 1 <= s <= 4:
                        dve_front(dve, b + 1, 1 - par, 2 * s - 1)

        def act_exp(act, b, s):
            attn, _ = group(s)
            width = P + T if attn == 0 else 2 * T
            g = b * STEPS + s
            for j in range(GH):
                act.wait_ge(shifted, GH * g + j + 1)
                if j == 0 and not (isinstance(g, int) and g < 2):
                    act.wait_ge(weighed, g - 1)
                nc.scalar.activation(probs[:, GH * (s % 2) + j, 0:width], bank_b[j % 2][:, 0:width], ACT.Exp,
                                     scale=SCALE).then_inc(exped, 1)
                yield

        def act_front(act, b, item):
            if item > 5:
                return
            act.wait_ge(front_filled, 8 * b + item + 1)
            if item == 0:
                nc.scalar.copy(xnT[:, :], bank_f[:, 0:T]).then_inc(front_act, 1)
            elif item == 3:
                nc.scalar.copy(ctxT[:, :], bank_f[0:CC, 0:T]).then_inc(front_act, 1)
            else:
                n = {1: Q, 2: K, 4: KC, 5: QC}[item]
                if not (isinstance(b, int) and b == 0):
                    act.wait_ge(stacked[n], 16 * 2 * len(PRODUCTS) * b)
                nc.scalar.activation(part[:, n, 0, :], bank_f[:, 0:T], ACT.Identity, bias=bqk_sb[:, n:n + 1])\
                    .then_inc(front_act, 1)

        def act_copy_max(act, b, s):
            g = b * STEPS + s
            act.wait_ge(m_turned, g + 1)
            if not (isinstance(g, int) and g < 2):
                act.wait_ge(m_placed[s % 2], 16 * (b * 4 + s // 2))
            nc.scalar.copy(mrows[:, s % 2, :], bank_m[0:3 * GH, 0:T]).then_inc(m_copied, 1)

        def act_copy_out(act, b, r):
            act.wait_ge(weighed, b * STEPS + 2 * r + 2)
            if not (isinstance(b, int) and b == 0 and r < 2):
                act.wait_ge(o_turned, b * 4 + r - 1)
            nc.scalar.copy(o_sb[:, r % 2, :], bank_o).then_inc(o_copied, 1)

        def act_copy_y(act, b):
            act.wait_ge(y_turned, b + 1)
            nc.scalar.copy(yT[:, :], bank_t[:, 0:T]).then_inc(y_copied, 1)

        def act_batch(act, b, par, first=False, last=False):
            for s in range(STEPS):
                e = act_exp(act, b, s)
                for j in range(GH):
                    next(e)
                    if j == 1:
                        if s % 2 == 0 and s > 0:
                            act_copy_out(act, b, s // 2 - 1)
                        elif s == 0 and not first:
                            act_copy_out(act, b - 1, 3)
                        if not last and 1 <= s <= 4:
                            act_front(act, b + 1, 2 * s - 2)
                    if j == 2:
                        if not (last and s + TURN >= STEPS):
                            tb, _, ts = later(b, par, s, TURN)
                            act_copy_max(act, tb, ts)
                        if s == 1 and not first:
                            act_copy_y(act, b - 1)
                    if j == 3 and not last and 1 <= s <= 4:
                        act_front(act, b + 1, 2 * s - 1)

        def pool_split_max(pool, b, s):
            g = b * STEPS + s
            n = 5 * g
            mp = mparts[:, s % 2]
            pool.wait_ge(maxed, GH * (g + 1))
            pool.nop(nofuse=True)
            nc.gpsimd.tensor_scalar(negmax[:, :, :], rowmax[:, s % 4], -1.0, None, ALU.mult).then_inc(msplit, 1)
            pool.wait_ge(msplit, n + 1)
            if not (isinstance(g, int) and g < 2):
                pool.wait_ge(m_turned, g - 1)
            pool.nop(nofuse=True)
            nc.gpsimd.tensor_copy(mp[:, :, 0, :], negmax[:, :, :]).then_inc(msplit, 1)
            pool.wait_ge(msplit, n + 2)
            nc.gpsimd.tensor_tensor(negres[:, :, :], negmax[:, :, :], mp[:, :, 0, :], ALU.subtract)\
                .then_inc(msplit, 1)
            pool.wait_ge(msplit, n + 3)
            pool.nop(nofuse=True)
            nc.gpsimd.tensor_copy(mp[:, :, 1, :], negres[:, :, :]).then_inc(msplit, 1)
            pool.wait_ge(msplit, n + 4)
            nc.gpsimd.tensor_tensor(mp[:, :, 2, :], negres[:, :, :], mp[:, :, 1, :], ALU.subtract)\
                .then_inc(msplit, 1)

        def pool_low(pool, b, n):
            pool.wait_ge(front_dve, 10 * b + 2 * n + 2)
            nc.gpsimd.tensor_tensor(part[:, n, 2, :], resid[:, n, :], part[:, n, 1, :], ALU.subtract)\
                .then_inc(low_done, 1)

        def pool_root(pool, b):
            pool.wait_ge(ln_step, 7 * b + 5)
            nc.gpsimd.tensor_tensor(rstd[:, :], vareps[:, :], minus_half[:, 0:QT], ALU.pow).then_inc(rooted, 1)

        def pool_weights(pool, e):
            nc.gpsimd.tensor_copy(w1_hi[:, e, :], w1_sb[:, e, :]).then_inc(w_hi_done, 1)
            nc.gpsimd.tensor_copy(w2_hi[:, e], w2_sb[:, e]).then_inc(w_hi_done, 1)
            pool.wait_ge(w_hi_done, 2 * e + 2)
            nc.gpsimd.tensor_tensor(w1_lo[:, e, :], w1_sb[:, e, :], w1_hi[:, e, :].bitcast(F32), ALU.subtract)\
                .then_inc(w_lo_done, 1)
            nc.gpsimd.tensor_tensor(w2_lo[:, e], w2_sb[:, e], w2_hi[:, e].bitcast(F32), ALU.subtract)\
                .then_inc(w_lo_done, 1)

        def pool_batch(pool, b, par, first=False, last=False):
            for s in range(STEPS):
                if s == 0 and not last:
                    pool_root(pool, b + 1)
                if not last and 2 <= s <= 5:
                    pool_low(pool, b + 1, s - 2)
                if not (last and s + LEAD >= STEPS):
                    ab, _, a_s = later(b, par, s, LEAD)
                    pool_split_max(pool, ab, a_s)
                if s == 6:
                    pool_weights(pool, b)

        def sp_place_max(sp, b, par, s):
            attn, h0 = group(s)
            sp.wait_ge(m_copied, b * STEPS + s + 1)
            sp.dma_start(qstack[ROWS:MROWS, par, attn, h0:h0 + GH, :], mrows[:, s % 2, :])\
                .then_inc(m_placed[s % 2], 16)

        def sp_stack(sp, b, par, n, which):
            attn = n // 2
            stack = qstack if n in (Q, QC) else kstack
            side = 0 if n in (Q, QC) else 1
            sp.wait_ge(front_act, 6 * b + {Q: 2, K: 3, KC: 5, QC: 6}[n])
            if which:
                sp.nop(nofuse=True)
                sp.wait_ge(low_done, 4 * b + n + 1)
            for c, parts in enumerate(PRODUCTS):
                p = parts[side]
                if (p > 0) != which:
                    continue
                for e in range(2):
                    rows = slice(HEAD_ROWS * e + D * c, HEAD_ROWS * e + D * (c + 1))
                    cols = slice(H // 2 * e, H // 2 * (e + 1)) if side == 0 else slice(0, H // 2)
                    sp.dma_start(stack[rows, par, attn, cols, :], part[64 * e:64 * (e + 1), n, p, :])\
                        .then_inc(stacked[n], 16)

        def sp_batch(sp, b, par, first=False, last=False):
            for s in range(STEPS):
                if s == 0 and not last:
                    if not first:
                        sp.wait_ge(front_filled, 8 * (b - 1) + 4)
                    sp.nop(nofuse=True)
                    sp.dma_start(ctx_sb[:, 1 - par, :, :], ctx_in[b + 1]).then_inc(ctx_loaded[1 - par], 16)
                if not (last and s + TURN >= STEPS):
                    sp_place_max(sp, *later(b, par, s, TURN))
                if last:
                    continue
                if s == 1:
                    sp.wait_ge(shifted, b * STEPS * GH + 1)
                    sp.nop(nofuse=True)
                    sp_stack(sp, b + 1, 1 - par, Q, False)
                elif s == 2:
                    sp_stack(sp, b + 1, 1 - par, K, False)
                    sp_stack(sp, b + 1, 1 - par, Q, True)
                elif s == 3:
                    sp_stack(sp, b + 1, 1 - par, K, True)
                    sp_stack(sp, b + 1, 1 - par, KC, False)
                    sp_stack(sp, b + 1, 1 - par, QC, False)
                elif s == 4:
                    sp_stack(sp, b + 1, 1 - par, KC, True)
                    sp_stack(sp, b + 1, 1 - par, QC, True)

        def batches(eng, run):
            run(eng, 0, 0, first=True)
            with eng.Fori(0, NB // 2 - 1) as i:
                run(eng, 2 * i + 1, 1)
                run(eng, 2 * i + 2, 0)
            run(eng, NB - 1, 1, last=True)

        with nc.Block() as block:
            @block.sync
            def _(sp):
                for dst, src in ((x_all[:, 0:QT, :], x[:, 0:QT, :]), (x_all[:, QT:, :], x[:, QT:, :])):
                    sp.dma_start(dst, src).then_inc(x_in, 16)
                for dst, src in ((wqk_sb[:, :, :], wqk), (bqk_sb[:, :], bqk), (wck_sb[:, :], wck),
                                 (wv_sb[:, :], wv), (wcv_sb[:, :], wcv), (wp_sb[:, :], wp),
                                 (bvp_sb[:, :, :], bvp.unsqueeze(0).to_broadcast([P, 3, C])),
                                 (gate_sb[:, :], gates.unsqueeze(0).to_broadcast([P, 2]))):
                    sp.dma_start(dst, src).then_inc(w_in, 16)
                sp.dma_start(ctx_sb[:, 0, :, :], ctx_in[0]).then_inc(ctx_loaded[0], 16)
                for dst, src in ((w1_sb[:, :, :], w1t), (w2_sb[:, :, :, :], w2t), (rw_sb[:, :], rwt)):
                    sp.dma_start(dst, src).then_inc(moe_in, 16)
                sp.wait_ge(const_dve, 1)
                for which in (False, True):
                    for n in range(4):
                        sp_stack(sp, 0, 0, n, which)
                for s in range(TURN):
                    sp_place_max(sp, 0, 0, s)
                batches(sp, sp_batch)

            @block.gpsimd
            def _(pool):
                n = 0
                for m, fill in ((ident, 0.0), (identb, 0.0), (mask_qk, 0.0), (mask_kq, 0.0)):
                    nc.gpsimd.memset(m[:, :], fill).then_inc(const_pool, 1)
                nc.gpsimd.memset(minus_half[:, :], -0.5).then_inc(const_pool, 1)
                pool.wait_ge(const_pool, 5)
                for m in (ident, identb):
                    nc.gpsimd.affine_select(out=m[:, :], in_=m[:, :], compare_op=ALU.not_equal, fill=1.0, base=0,
                                            pattern=[[-1, P]], channel_multiplier=1).then_inc(const_pool, 1)
                nc.gpsimd.affine_select(out=mask_qk[:, :], in_=mask_qk[:, :], compare_op=ALU.is_ge, fill=MASKED,
                                        base=0, pattern=[[-1, P]], channel_multiplier=1).then_inc(const_pool, 1)
                nc.gpsimd.affine_select(out=mask_kq[:, :], in_=mask_kq[:, :], compare_op=ALU.is_ge, fill=MASKED,
                                        base=0, pattern=[[1, P]], channel_multiplier=-1).then_inc(const_pool, 1)
                pool_root(pool, 0)
                for i in range(4):
                    pool_low(pool, 0, i)
                for s in range(LEAD):
                    pool_split_max(pool, 0, s)
                pool.wait_ge(moe_in, 48)
                batches(pool, pool_batch)

            @block.scalar
            def _(act):
                act.wait_ge(w_in, 16 * 8)
                nc.scalar.activation(tgate[:, :], gate_sb[:, :], ACT.Tanh).then_inc(gate_done, 1)
                for item in range(8):
                    act_front(act, 0, item)
                for s in range(TURN):
                    act_copy_max(act, 0, s)
                batches(act, act_batch)
                act_copy_out(act, NB - 1, 3)
                act_copy_y(act, NB - 1)

            @block.vector
            def _(dve):
                nc.vector.memset(qstack[:, :, :, :, :].rearrange("p a b h t -> p (a b h t)").bitcast(mybir.dt.uint32),
                                 0).then_inc(const_dve, 1)
                nc.vector.memset(kstack[ROWS:MROWS, :, :, :, :], 1.0).then_inc(const_dve, 1)
                nc.vector.memset(vext[:, :, :, :, :, D:D + 1], 1.0).then_inc(const_dve, 1)
                nc.vector.memset(vext[:, :, :, :, :, 0:D], 0.0).then_inc(const_dve, 1)
                nc.vector.memset(vext[:, :, :, :, :, D + 1:], 0.0).then_inc(const_dve, 1)
                dve.wait_ge(const_dve, 5)
                dve.wait_ge(x_in, 32)
                dve.wait_ge(w_in, 16 * 8)
                dve.wait_ge(gate_done, 1)
                dve_norm_x(dve, 0)
                for item in range(8):
                    dve_front(dve, 0, 0, item)
                for s in range(LEAD):
                    for _step in dve_max(dve, 0, s):
                        pass
                batches(dve, dve_batch)
                dve_norm_out(dve, NB - 1, 3)
                dve_residual(dve, NB - 1)

            @block.tensor
            def _(pe):
                pe.wait_ge(const_pool, 9)
                pe.wait_ge(const_dve, 5)
                pe.wait_ge(w_in, 16 * 8)
                for item in range(8):
                    pe_front(pe, 0, 0, item)
                for s in range(LEAD):
                    for _step in pe_scores(pe, 0, 0, s):
                        pass
                    if s > 0:
                        pe_turn_max(pe, 0, s - 1)
                batches(pe, pe_batch)
                pe_weigh(pe, NB - 1, 1, STEPS - 1)
                pe_turn_out(pe, NB - 1, 3)
                pe_turn_y(pe, NB - 1)
                pe_project(pe, NB - 1)

        attention.close()
        experts(nc, es, x_all, tgate, ident, identb, w1_hi, w1_lo, w2_hi, w2_lo, rw_sb,
                minus_half, psum, out)


def experts(nc, es, x_all, tgate, ident, identb, w_hi, w_lo, w2_hi, w2_lo, rw_sb, minus_half,
            psum, out):
    def sb(name, shape, dt=F32):
        return es.enter_context(nc.sbuf_tensor(name, shape, dt))

    def sem(name):
        return es.enter_context(nc.semaphore(name))

    NTOK = NB * T
    xn2 = sb("xn2", [P, CT, C])
    stats2 = sb("stats2", [P, CT, 6])
    meanvar2 = sb("meanvar2", [P, CT, 2])
    vareps2 = sb("vareps2", [P, CT])
    rstd2 = sb("rstd2", [P, CT])
    x_t = sb("x_t", [P, CHUNK])
    x_hi = sb("x_hi", [P, NTOK], F32R)
    x_lo = sb("x_lo", [P, NTOK], F32R)
    logit = sb("logit", [P, CT, NE])
    top = sb("top", [P, CT])
    total = sb("total", [P, CT])
    expo = sb("expo", [P, CT, NE])
    prob = sb("prob", [P, CT, NE])
    earlier = sb("earlier", [P, NE, NE])
    above = sb("above", [P, CT, NE, NE])
    ties = sb("ties", [P, CT, NE, NE])
    rank = sb("rank", [P, CT, NE])
    comb = sb("comb", [P, CT, NE])
    combres = sb("combres", [P, CT, NE])
    combparts = sb("combparts", [P, CT, 3, NE], BF16)
    comb_t = sb("comb_t", [3 * NE, NTOK], BF16)
    pick = sb("pick", [3 * NE, NE, P], BF16)
    silu = sb("silu", [P, IT, CHUNK])
    gated = sb("gated", [P, IT, CHUNK])
    y = sb("y", [P, 2, IT, CHUNK])
    y_hi = sb("y_hi", [P, 2, IT, CHUNK], F32R)
    y_lo = sb("y_lo", [P, 2, IT, CHUNK], F32R)
    out_t = sb("out_t", [P, CHUNK])

    bank_gate = [psum[:, k, :] for k in range(IT)]
    bank_up = [psum[:, IT + k, :] for k in range(IT)]
    bank_comb = psum[:, 4, :]
    bank_out = psum[:, 5, :]
    bank_turn = psum[:, 6, :]
    bank_route = psum[:, 7, :]

    consts = sem("consts")
    norm_step, rooted2 = sem("norm_step"), sem("rooted2")
    x_turned, x_rounded, x_copied, x_split = sem("x_turned"), sem("x_rounded"), sem("x_copied"), sem("x_split")
    routed, shifted_logits, expo_done, route_step = sem("routed"), sem("shifted_logits"), sem("expo_done"), sem("route_step")
    comb_step, comb_turned, comb_copied = sem("comb_step"), sem("comb_turned"), sem("comb_copied")
    comb_spread, comb_read = sem("comb_spread"), sem("comb_read")
    gate_ready, gate_read = sem("gate_ready"), sem("gate_read")
    up_ready, up_read = sem("up_ready"), sem("up_read")
    y_ready, y_rounded, y_split = sem("y_ready"), sem("y_rounded"), sem("y_split")
    gated_done = sem("gated_done")
    down_done = sem("down_done")
    out_ready, out_copied, out_turned, out_added, stored = (
        sem("out_ready"), sem("out_copied"), sem("out_turned"), sem("out_added"), sem("stored"))
    ROUTE = 12
    NORM = 2 * CT + 1 + CT

    with nc.Block() as block:
        @block.gpsimd
        def _(pool):
            nc.gpsimd.memset(pick[:, :, :], 0.0).then_inc(consts, 1)
            pool.wait_ge(consts, 1)
            for c in range(3):
                nc.gpsimd.affine_select(out=pick[:, :, :], in_=pick[:, :, :], compare_op=ALU.not_equal, fill=1.0,
                                        base=-NE * c, pattern=[[-1, NE], [0, P]], channel_multiplier=1)\
                    .then_inc(consts, 1)
                pool.wait_ge(consts, 2 + c)
            nc.gpsimd.memset(earlier[:, :, :], 1.0).then_inc(consts, 1)
            pool.wait_ge(consts, 5)
            nc.gpsimd.affine_select(out=earlier[:, :, :], in_=earlier[:, :, :], compare_op=ALU.is_ge, fill=0.0,
                                    base=-1, pattern=[[1, NE], [-1, NE]], channel_multiplier=0).then_inc(consts, 1)
            with pool.Fori(0, NCHUNK) as c:
                pool.wait_ge(norm_step, NORM * c + 2 * CT + 1)
                nc.gpsimd.tensor_tensor(rstd2[:, :], vareps2[:, :], minus_half[:, :], ALU.pow).then_inc(rooted2, 1)
                pool.wait_ge(x_rounded, c + 1)
                pool.wait_ge(x_copied, c + 1)
                nc.gpsimd.tensor_tensor(x_lo[:, bass.ds(c * CHUNK, CHUNK)], x_t[:, :],
                                        x_hi[:, bass.ds(c * CHUNK, CHUNK)].bitcast(F32), ALU.subtract)\
                    .then_inc(x_split, 1)
            pool.nop().then_inc(y_split, 4)
            with pool.Fori(0, NCHUNK) as c:
                for e in range(NE):
                    for k in range(IT):
                        n = (c * NE + e) * IT + k
                        pool.wait_ge(y_rounded, n + 1)
                        pool.wait_ge(down_done, n + 1)
                        nc.gpsimd.tensor_tensor(y_lo[:, e % 2, k, :], y[:, e % 2, k, :],
                                                y_hi[:, e % 2, k, :].bitcast(F32), ALU.subtract).then_inc(y_split, 1)

        @block.scalar
        def _(act):
            with act.Fori(0, NCHUNK) as c:
                act.wait_ge(x_turned, c + 1)
                nc.scalar.copy(x_hi[:, bass.ds(c * CHUNK, CHUNK)], bank_turn).then_inc(x_rounded, 1)
                act.wait_ge(shifted_logits, c + 1)
                nc.scalar.activation(expo[:, :, :], logit[:, :, :], ACT.Exp).then_inc(expo_done, 1)
            act.nop().then_inc(gate_read, 2)
            act.nop().then_inc(out_copied, 1)
            with act.Fori(0, NCHUNK) as c:
                def round_y(e, k):
                    n = (c * NE + e) * IT + k
                    act.wait_ge(y_ready, n + 1)
                    act.wait_ge(down_done, n + 1)
                    nc.scalar.copy(y_hi[:, e % 2, k, :], y[:, e % 2, k, :]).then_inc(y_rounded, 1)

                for e in range(NE):
                    for k in range(IT):
                        n = (c * NE + e) * IT + k
                        act.wait_ge(gate_ready, n + 1)
                        act.wait_ge(up_read, n + 1)
                        nc.scalar.activation(silu[:, k, :], bank_gate[k], ACT.Silu).then_inc(gate_read, 1)
                        if k == 1:
                            round_y(e, 0)
                        elif e > 0:
                            round_y(e - 1, 1)
                round_y(NE - 1, 1)
                act.wait_ge(out_ready, c + 1)
                act.wait_ge(out_turned, c + 1)
                nc.scalar.copy(out_t[:, :], bank_out).then_inc(out_copied, 1)

        @block.vector
        def _(dve):
            dve.wait_ge(consts, 6)
            with dve.Fori(0, NCHUNK) as c:
                for t in range(CT):
                    nc.vector.bn_stats(stats2[:, t, :], x_all[:, CT * c + t, :]).then_inc(norm_step, 1)
                for t in range(CT):
                    dve.wait_ge(norm_step, NORM * c + 1 + t)
                    dve.nop(nofuse=True)
                    nc.vector.bn_aggr(meanvar2[:, t, :], stats2[:, t, :]).then_inc(norm_step, 1)
                dve.wait_ge(norm_step, NORM * c + 2 * CT)
                nc.vector.tensor_scalar(vareps2[:, :], meanvar2[:, :, 1], EPS, None, ALU.add).then_inc(norm_step, 1)
                dve.wait_ge(rooted2, c + 1)
                for t in range(CT):
                    nc.vector.tensor_scalar(xn2[:, t, :], x_all[:, CT * c + t, :], meanvar2[:, t, 0:1],
                                            rstd2[:, t:t + 1], ALU.subtract, ALU.mult).then_inc(norm_step, 1)
                dve.wait_ge(x_rounded, c + 1)
                nc.vector.tensor_copy(x_t[:, :], bank_turn).then_inc(x_copied, 1)
                step = ROUTE * c
                dve.wait_ge(routed, c + 1)
                r = bank_route[:, 0:CT * NE].rearrange("p (t e) -> p t e", e=NE)
                nc.vector.tensor_reduce(top[:, :], r, AX_X, ALU.max).then_inc(route_step, 1)
                dve.wait_ge(route_step, step + 1)
                nc.vector.tensor_tensor(logit[:, :, :], r, top[:, :].unsqueeze(2).to_broadcast([P, CT, NE]),
                                        ALU.subtract).then_inc(shifted_logits, 1)
                dve.wait_ge(expo_done, c + 1)
                nc.vector.tensor_reduce(top[:, :], expo[:, :, :], AX_X, ALU.add).then_inc(route_step, 1)
                dve.wait_ge(route_step, step + 2)
                nc.vector.reciprocal(total[:, :], top[:, :]).then_inc(route_step, 1)
                dve.wait_ge(route_step, step + 3)
                nc.vector.tensor_tensor(prob[:, :, :], expo[:, :, :],
                                        total[:, :].unsqueeze(2).to_broadcast([P, CT, NE]), ALU.mult)\
                    .then_inc(route_step, 1)
                dve.wait_ge(route_step, step + 4)
                other = prob[:, :, :].unsqueeze(2).to_broadcast([P, CT, NE, NE])
                own = prob[:, :, :].unsqueeze(3).to_broadcast([P, CT, NE, NE])
                nc.vector.tensor_tensor(above[:, :, :, :], other, own, ALU.is_gt).then_inc(route_step, 1)
                nc.vector.tensor_tensor(ties[:, :, :, :], other, own, ALU.is_ge).then_inc(route_step, 1)
                dve.wait_ge(route_step, step + 6)
                nc.vector.tensor_tensor(ties[:, :, :, :], ties[:, :, :, :],
                                        earlier[:, :, :].unsqueeze(1).to_broadcast([P, CT, NE, NE]), ALU.mult)\
                    .then_inc(route_step, 1)
                dve.wait_ge(route_step, step + 7)
                nc.vector.tensor_tensor(above[:, :, :, :], above[:, :, :, :], ties[:, :, :, :], ALU.max)\
                    .then_inc(route_step, 1)
                dve.wait_ge(route_step, step + 8)
                nc.vector.tensor_reduce(rank[:, :, :], above[:, :, :, :], AX_X, ALU.add).then_inc(route_step, 1)
                dve.wait_ge(route_step, step + 9)
                nc.vector.scalar_tensor_tensor(out=comb[:, :, :], in0=rank[:, :, :], scalar=float(TOPK),
                                               in1=prob[:, :, :], op0=ALU.is_lt, op1=ALU.mult)\
                    .then_inc(route_step, 1)
                dve.wait_ge(route_step, step + 10)
                nc.vector.tensor_copy(combparts[:, :, 0, :], comb[:, :, :]).then_inc(route_step, 1)
                dve.wait_ge(route_step, step + 11)
                nc.vector.tensor_tensor(combres[:, :, :], comb[:, :, :], combparts[:, :, 0, :], ALU.subtract)\
                    .then_inc(route_step, 1)
                dve.wait_ge(route_step, step + 12)
                nc.vector.tensor_copy(combparts[:, :, 1, :], combres[:, :, :]).then_inc(comb_step, 1)
                dve.wait_ge(comb_step, 2 * c + 1)
                nc.vector.tensor_tensor(combparts[:, :, 2, :], combres[:, :, :], combparts[:, :, 1, :],
                                        ALU.subtract).then_inc(comb_step, 1)
                dve.wait_ge(comb_turned, c + 1)
                nc.vector.tensor_copy(comb_t[:, bass.ds(c * CHUNK, CHUNK)],
                                      bank_comb.bitcast(BF16)[0:3 * NE, 0:CHUNK]).then_inc(comb_copied, 1)
            dve.nop().then_inc(up_read, 2)
            dve.nop().then_inc(comb_read, 1)
            dve.nop().then_inc(out_added, 1)
            with dve.Fori(0, NCHUNK) as c:
                for e in range(NE):
                    for k in range(IT):
                        n = (c * NE + e) * IT + k
                        dve.wait_ge(up_ready, n + 1)
                        dve.wait_ge(gate_read, n + 3)
                        nc.vector.tensor_tensor(gated[:, k, :], silu[:, k, :], bank_up[k], ALU.mult)\
                            .then_inc(up_read, 1)
                        dve.wait_ge(up_read, n + 3)
                        dve.wait_ge(comb_spread, c * NE + e + 1)
                        dve.wait_ge(y_split, n + 1)
                        op = nc.vector.tensor_tensor(y[:, e % 2, k, :], gated[:, k, :], bank_comb, ALU.mult)
                        op.then_inc(y_ready, 1)
                    dve.wait_ge(y_ready, (c * NE + e + 1) * IT)
                    dve.sem_inc(comb_read, 1)
                dve.wait_ge(out_turned, c + 2)
                for t in range(CT):
                    op = nc.vector.scalar_tensor_tensor(out=x_all[:, CT * c + t, :], in0=bank_turn[:, P * t:P * (t + 1)],
                                                        scalar=tgate[:, 1:2], in1=x_all[:, CT * c + t, :],
                                                        op0=ALU.mult, op1=ALU.add)
                op.then_inc(out_added, 1)

        @block.tensor
        def _(pe):
            with pe.Fori(0, NCHUNK) as c:
                pe.wait_ge(norm_step, NORM * (c + 1))
                for t in range(CT):
                    mm = nc.tensor.transpose(bank_turn[:, P * t:P * (t + 1)], xn2[:, t, :], ident[:, :])
                mm.then_inc(x_turned, 1)
                pe.wait_ge(x_copied, c + 1)
                for t in range(CT):
                    mm = nc.tensor.matmul(bank_route[:, NE * t:NE * (t + 1)], x_t[:, P * t:P * (t + 1)], rw_sb[:, :],
                                          start=True, stop=True)
                mm.then_inc(routed, 1)
                pe.wait_ge(comb_step, 2 * c + 2)
                pe.nop(nofuse=True)
                for t in range(CT):
                    mm = nc.tensor.transpose(bank_comb.bitcast(BF16)[0:3 * NE, P * t:P * (t + 1)],
                                             combparts[:, t, :, :].rearrange("p c e -> p (c e)"), identb[:, :])
                mm.then_inc(comb_turned, 1)
            pe.wait_ge(comb_copied, NCHUNK)
            pe.wait_ge(x_split, NCHUNK)
            pe.nop().then_inc(down_done, 4)
            pe.nop().then_inc(out_turned, 1)
            with pe.Fori(0, NCHUNK) as c:
                tok = bass.ds(c * CHUNK, CHUNK)

                def up(e, k):
                    n = (c * NE + e) * IT + k
                    for bank, col, read, ready in ((bank_gate[k], P * k, gate_read, gate_ready),
                                                   (bank_up[k], INTER + P * k, up_read, up_ready)):
                        pe.wait_ge(read, n + 1)
                        for i, (w, xx) in enumerate(((w_hi, x_hi), (w_hi, x_lo), (w_lo, x_hi))):
                            mm = nc.tensor.matmul(bank, w[:, e, col:col + P], xx[:, tok], start=i == 0, stop=i == 2)
                        mm.then_inc(ready, 1)

                def down(e, k):
                    n = (c * NE + e) * IT + k
                    pe.wait_ge(y_split, n + 5)
                    if e == 0 and k == 0:
                        pe.wait_ge(out_copied, c + 1)
                    for i, (w, yy) in enumerate(((w2_hi, y_hi), (w2_hi, y_lo), (w2_lo, y_hi))):
                        mm = nc.tensor.matmul(bank_out, w[:, e, k, :], yy[:, e % 2, k, :],
                                              start=e + k + i == 0, stop=e == NE - 1 and k == IT - 1 and i == 2)
                    mm.then_inc(down_done, 1)

                for e in range(NE):
                    pe.wait_ge(comb_read, c * NE + e + 1)
                    pe.nop(nofuse=True)
                    nc.tensor.matmul(bank_comb, pick[:, e, :], comb_t[:, tok], start=True, stop=True)\
                        .then_inc(comb_spread, 1)
                    for k in range(IT):
                        up(e, k)
                        if e > 0:
                            down(e - 1, k)
                for k in range(IT):
                    down(NE - 1, k)
                pe.wait_ge(down_done, (c + 1) * NE * IT + 4)
                pe.sem_inc(out_ready, 1)
                pe.wait_ge(out_copied, c + 2)
                pe.wait_ge(out_added, c + 1)
                for t in range(CT):
                    mm = nc.tensor.transpose(bank_turn[:, P * t:P * (t + 1)], out_t[:, P * t:P * (t + 1)], ident[:, :])
                mm.then_inc(out_turned, 1)

        @block.sync
        def _(sp):
            with sp.Fori(0, NCHUNK) as c:
                sp.wait_ge(out_added, c + 2)
                sp.nop(nofuse=True)
                sp.dma_start(out[:, bass.ds(c * CT, CT), :], x_all[:, bass.ds(c * CT, CT), :]).then_inc(stored, 16)
            sp.wait_ge(stored, 16 * NCHUNK)


def kernel(**inputs):
    import numpy as np
    from concourse import bacc
    from concourse.bass_utils import run_bass_kernel_spmd

    def a(name):
        return np.asarray(inputs[name])

    def turned(w):
        return np.ascontiguousarray(w.reshape(*w.shape[:-1], 2, H // 2, D).swapaxes(-1, -2).reshape(w.shape))

    x = "L0_xattn_"
    tiles = lambda t: t.reshape(NB, QT, P, t.shape[-1])
    arrays = {
        "x": np.ascontiguousarray(a("x").reshape(NTILE, P, C).transpose(1, 0, 2)),
        "ctx_in": np.ascontiguousarray(tiles(a("ctx_512")).transpose(0, 2, 1, 3)),
        "gates": np.concatenate([a("g_xattn"), a("g_ffn")]),
        "wqk": np.ascontiguousarray(np.stack([turned(a(x + n)) for n in ("Wq", "Wk", "Wcq")], 1)),
        "wck": turned(a(x + "Wck")),
        "bqk": np.ascontiguousarray(np.stack([turned(a(x + n)) for n in ("bq", "bk", "bck", "bcq")], 1)),
        "wv": a(x + "Wv"), "wcv": a(x + "Wcv"), "wp": a(x + "Wp"),
        "bvp": np.stack([a(x + n) for n in ("bv", "bcv", "bp")]),
        "w1t": np.ascontiguousarray(a("L0_ffn_w1").transpose(2, 0, 1)),
        "w2t": np.ascontiguousarray(a("L0_ffn_w2").reshape(NE, C, IT, P).transpose(3, 0, 2, 1)),
        "rwt": np.ascontiguousarray(a("L0_ffn_router_w").T),
    }
    nc = bacc.Bacc("TRN2", target_bir_lowering=False, num_devices=1)
    args = {n: nc.dram_tensor(n, v.shape, mybir.dt.from_np(v.dtype), kind="ExternalInput").ap()
            for n, v in arrays.items()}
    args["out"] = nc.dram_tensor("out", (P, NTILE, C), F32, kind="ExternalOutput").ap()
    gated_attention_experts(nc, **args)
    r = run_bass_kernel_spmd(nc, [arrays], core_ids=[0])
    return r.results[0]["out"].transpose(1, 0, 2).reshape(NB, T, C)
```

```python
from contextlib import ExitStack

import concourse.bass as bass
from concourse import mybir

F32 = mybir.dt.float32
F32R = mybir.dt.float32r
BF16 = mybir.dt.bfloat16
ALU = mybir.AluOpType
ACT = mybir.ActivationFunctionType
AX_X = mybir.AxisListType.X

P = 128
NB, T, C = 8, 256, 128
CC = 64
H, D = 16, 8
QT = T // P
NTILE = NB * QT
STEPS = 8
GH = 4
QUAD = P // GH
SCALE = float(D) ** -0.5
MASKED = -1e30
BF16_ONES = 0x3F803F80
EPS = 1e-5
NP = 3
PART_ROWS = NP * D
ROWS = 96
MROWS = ROWS + 3
Q, K, QC, KC = range(4)
NE, INTER, TOPK = 8, 256, 2
CHUNK = 512
NCHUNK = NB * T // CHUNK
CT = CHUNK // P
IT = INTER // P
WCOLS = 2 * INTER + IT * C


def gated_attention_experts(nc, x, ctx_in, gates, wqk, wck, bqk, wv, wcv, wp, bvp, w12t, rwt, scratch, out):
    with ExitStack() as es, ExitStack() as attention:
        def kept(name, shape, dt=F32):
            return es.enter_context(nc.sbuf_tensor(name, shape, dt))

        def sb(name, shape, dt=F32):
            return attention.enter_context(nc.sbuf_tensor(name, shape, dt))

        def sem(name):
            return es.enter_context(nc.semaphore(name))

        x_all = kept("x_all", [P, NTILE, C])
        tgate = kept("tgate", [P, 2])
        ident = kept("ident", [P, P])
        identb = kept("identb", [P, P], BF16)
        minus_half = kept("minus_half", [P, CT])
        w_hi = kept("w_hi", [P, NE, WCOLS], F32R)
        w_lo = kept("w_lo", [P, NE, WCOLS], F32R)
        rw_sb = kept("rw_sb", [P, NE])
        w_stage = sb("w_stage", [P, WCOLS])
        wqk_sb = sb("wqk_sb", [P, 3, C])
        wck_sb = sb("wck_sb", [CC, C])
        bqk_sb = sb("bqk_sb", [P, 4])
        wv_sb = sb("wv_sb", [P, C])
        wcv_sb = sb("wcv_sb", [CC, C])
        wp_sb = sb("wp_sb", [P, C])
        bvp_sb = sb("bvp_sb", [P, 3, C])
        gate_sb = sb("gate_sb", [P, 2])
        mask_qk = sb("mask_qk", [P, P], BF16)
        mask_kq = sb("mask_kq", [P, P], BF16)
        qstack = sb("qstack", [MROWS, 2, 2, H, T], BF16)
        kstack = sb("kstack", [MROWS, 2, 2, H, T], BF16)
        vext = sb("vext", [P, 2, 2, QT, H, QUAD])
        xn = sb("xn", [P, QT, C])
        xnT = sb("xnT", [P, T])
        ctxT = sb("ctxT", [CC, 2, T])
        stats = sb("stats", [P, QT, 6])
        meanvar = sb("meanvar", [P, QT, 2])
        vareps = sb("vareps", [P, QT])
        rstd = sb("rstd", [P, QT])
        part = sb("part", [P, 4, 3, T], BF16)
        resid = sb("resid", [P, 4, T])
        rowmax = sb("rowmax", [P, 4, QT, GH])
        negmax = sb("negmax", [P, QT, GH])
        negres = sb("negres", [P, QT, GH])
        mparts = sb("mparts", [P, 2, QT, 3, GH], BF16)
        mrows = sb("mrows", [3 * GH, 2, T], BF16)
        probs = sb("probs", [P, 2 * GH, 2 * T])
        o_sb = sb("o_sb", [P, 2, 2 * T])
        rden = sb("rden", [P, 2, QT, GH])
        ynorm = sb("ynorm", [P, 2, QT, GH, D])
        y_sb = sb("y_sb", [P, QT, C])
        yT = sb("yT", [P, T])
        proj_b = sb("proj_b", [P, QT, C])

        psum = es.enter_context(nc.psum_tensor("psum", [P, 8, 512], F32))
        bank_a = [psum[:, 0, :], psum[:, 1, :]]
        bank_b = [psum[:, 2, :], psum[:, 3, :]]
        bank_o = psum[:, 4, :]
        bank_t = psum[:, 5, :]
        bank_f = psum[:, 6, :]
        bank_m = psum[:, 7, :].bitcast(BF16)

        x_in, qk_in, w_in, rest_in = sem("x_in"), sem("qk_in"), sem("w_in"), sem("rest_in")
        ctx_loaded = [sem("ctx_loaded0"), sem("ctx_loaded1")]
        const_pool, const_dve = sem("const_pool"), sem("const_dve")
        gate_done = sem("gate_done")
        ln_step = sem("ln_step")
        rooted = sem("rooted")
        front_filled = sem("front_filled")
        front_act = sem("front_act")
        front_dve = sem("front_dve")
        low_done = sem("low_done")
        parts_out = [sem(f"parts_out{n}") for n in range(4)]
        stacked = [sem(f"stacked{n}") for n in range(4)]
        scored = sem("scored")
        maxed = sem("maxed")
        msplit = sem("msplit")
        m_turned = sem("m_turned")
        m_copied = sem("m_copied")
        m_placed = [sem("m_placed0"), sem("m_placed1")]
        shifted = sem("shifted")
        exped = sem("exped")
        weighed = sem("weighed")
        o_copied = sem("o_copied")
        o_turned = sem("o_turned")
        normed = sem("normed")
        y_turned, y_copied, projected = sem("y_turned"), sem("y_copied"), sem("projected")
        x1_step = sem("x1_step")
        w_staged = sem("w_staged")
        w_hi_done = sem("w_hi_done")
        w_lo_done = sem("w_lo_done")

        def group(s):
            return s % 2, GH * (s // 2)

        LEAD, TURN = 3, 2
        FRONT_SLOTS = [(0, 3), (1, 0), (1, 2), (2, 0), (2, 2), (3, 0), (3, 2)]

        def pe_scores(pe, b, par, s):
            attn, h0 = group(s)
            for j in range(GH):
                if s == attn and j == 0:
                    pe.wait_ge(stacked[QC if attn else Q], 16 * NP * (b + 1))
                    pe.wait_ge(stacked[KC if attn else K], 16 * (b + 1))
                yield
                u = (b * STEPS + s) * GH + j
                if not (isinstance(u, int) and u < 2):
                    pe.wait_ge(maxed, u - 1)
                q = qstack[0:ROWS, par, attn, h0 + j, :]
                k = kstack[0:ROWS, par, attn, h0 + j, :]
                a = bank_a[j % 2]
                if attn == 0:
                    nc.tensor.matmul(a[:, 0:P], q[:, 0:P], k[:, 0:P], start=True, stop=False)
                    nc.tensor.matmul(a[:, 0:P], identb[:, :], mask_qk[:, :], start=False, stop=True)
                    nc.tensor.matmul(a[:, P:P + T], q[:, P:T], k[:, :], start=True, stop=True)
                    mm = nc.tensor.matmul(a[:, T:T + P], identb[:, :], mask_qk[:, :], start=False, stop=True,
                                          skip_group_check=True)
                else:
                    nc.tensor.matmul(a[:, 0:T], q[:, 0:P], k[:, :], start=True, stop=True)
                    mm = nc.tensor.matmul(a[:, T:2 * T], q[:, P:T], k[:, :], start=True, stop=True)
                mm.then_inc(scored, 1)
                yield

        def pe_shifted(pe, b, par, s):
            attn, h0 = group(s)
            for j in range(GH):
                if j == 0:
                    pe.wait_ge(m_placed[s % 2], 16 * (b * 4 + s // 2 + 1))
                u = (b * STEPS + s) * GH + j
                if not (isinstance(u, int) and u < 2):
                    pe.wait_ge(exped, u - 1)
                q = qstack[0:MROWS, par, attn, h0 + j, :]
                k = kstack[0:MROWS, par, attn, h0 + j, :]
                s_b = bank_b[j % 2]
                if attn == 0:
                    nc.tensor.matmul(s_b[:, 0:T], k[:, 0:P], q[:, :], start=True, stop=True)
                    nc.tensor.matmul(s_b[:, 0:P], identb[:, :], mask_kq[:, :], start=False, stop=True,
                                     skip_group_check=True)
                    nc.tensor.matmul(s_b[:, T:T + P], k[:, P:T], q[:, P:T], start=True, stop=False)
                    mm = nc.tensor.matmul(s_b[:, T:T + P], identb[:, :], mask_kq[:, :], start=False, stop=True)
                else:
                    nc.tensor.matmul(s_b[:, 0:T], k[:, 0:P], q[:, :], start=True, stop=True)
                    mm = nc.tensor.matmul(s_b[:, T:2 * T], k[:, P:T], q[:, :], start=True, stop=True)
                mm.then_inc(shifted, 1)
                yield

        def pe_weigh(pe, b, par, s):
            attn, h0 = group(s)
            g = b * STEPS + s
            pe.wait_ge(exped, GH * (g + 1))
            if s == 0:
                pe.wait_ge(front_dve, 10 * (b + 1))
            if attn == 0 and not (isinstance(g, int) and g == 0):
                pe.wait_ge(o_copied, b * 4 + s // 2)
            for key_tile in range(QT):
                for j in range(GH):
                    first = key_tile == 0
                    skip = P if attn == 0 and not first else 0
                    pr = probs[:, GH * (s % 2) + j, T * key_tile:T * (key_tile + 1) - skip]
                    mm = nc.tensor.matmul(bank_o[QUAD * j:QUAD * (j + 1), T * attn + skip:T * (attn + 1)],
                                          vext[:, par, attn, key_tile, h0 + j, :], pr, start=first,
                                          stop=True, skip_group_check=True)
                if not first:
                    mm.then_inc(weighed, 1)
                yield

        def pe_turn_max(pe, b, s):
            g = b * STEPS + s
            pe.wait_ge(msplit, 5 * (g + 1))
            if not (isinstance(g, int) and g == 0):
                pe.wait_ge(m_copied, g)
            for t in range(QT):
                mm = nc.tensor.transpose(bank_m[0:3 * GH, P * t:P * (t + 1)],
                                         mparts[:, s % 2, t, :, :].rearrange("p c h -> p (c h)"), identb[:, :])
            mm.then_inc(m_turned, 1)

        def pe_turn_out(pe, b, r):
            pair = b * 4 + r
            pe.wait_ge(o_copied, pair + 1)
            if r == 0 and not (isinstance(b, int) and b == 0):
                pe.wait_ge(x1_step, 2 * b)
            if r > 0:
                pe.wait_ge(normed, 3 * pair)
            for n in range(4):
                mm = nc.tensor.transpose(bank_t[:, P * n:P * (n + 1)], o_sb[:, r % 2, P * n:P * (n + 1)],
                                         ident[:, :])
            mm.then_inc(o_turned, 1)

        def pe_turn_y(pe, b):
            pe.wait_ge(normed, 3 * 4 * (b + 1))
            for t in range(QT):
                mm = nc.tensor.transpose(bank_t[:, P * t:P * (t + 1)], y_sb[:, t, :], ident[:, :])
            mm.then_inc(y_turned, 1)

        def pe_project(pe, b):
            pe.wait_ge(y_copied, b + 1)
            for t in range(QT):
                mm = nc.tensor.matmul(bank_t[:, P * t:P * (t + 1)], yT[:, P * t:P * (t + 1)], wp_sb[:, :],
                                      start=True, stop=True)
            mm.then_inc(projected, 1)

        def pe_front(pe, b, par, item):
            if item == 0:
                if not isinstance(b, int) or b > 0:
                    pe.wait_ge(front_dve, 10 * b)
                pe.wait_ge(ln_step, 7 * (b + 1))
                for t in range(QT):
                    mm = nc.tensor.transpose(bank_f[:, P * t:P * (t + 1)], xn[:, t, :], ident[:, :])
            elif item <= 4:
                n = item - 1
                if n == 0:
                    pe.wait_ge(front_act, 5 * b + 1)
                else:
                    pe.wait_ge(front_dve, 10 * b + 2 * n - 1)
                if n == KC:
                    pe.wait_ge(ctx_loaded[par], 8 * (b - par) + 16)
                    pe.nop(nofuse=True)
                w, src = (wck_sb, ctxT[:, par, :]) if n == KC else (wqk_sb[:, n, :], xnT)
                mm = nc.tensor.matmul(bank_f[:, 0:T], w[:, :], src[:, :], start=True, stop=True)
            else:
                pe.wait_ge(front_dve, 10 * b + (7 if item == 5 else 9))
                src, w = (xnT, wv_sb) if item == 5 else (ctxT[:, par, :], wcv_sb)
                for t in range(QT):
                    mm = nc.tensor.matmul(bank_f[:, P * t:P * (t + 1)], src[:, P * t:P * (t + 1)], w[:, :],
                                          start=True, stop=True)
            mm.then_inc(front_filled, 1)

        def later(b, par, s, by):
            return (b, par, s + by) if s + by < STEPS else (b + 1, 1 - par, s + by - STEPS)

        def pe_batch(pe, b, par, first=False, last=False):
            for s in range(STEPS):
                ahead = None if last and s + LEAD >= STEPS else pe_scores(pe, *later(b, par, s, LEAD))
                shift = pe_shifted(pe, b, par, s)
                weigh = None
                if s > 0:
                    weigh = pe_weigh(pe, b, par, s - 1)
                elif not first:
                    weigh = pe_weigh(pe, b - 1, 1 - par, STEPS - 1)
                for j in range(GH):
                    next(shift)
                    if ahead:
                        next(ahead)
                        next(ahead)
                    if j == 0 and s == 2 and not first:
                        pe_project(pe, b - 1)
                    if j < QT and weigh:
                        next(weigh)
                    if not last and (s, j) in FRONT_SLOTS:
                        pe_front(pe, b + 1, 1 - par, FRONT_SLOTS.index((s, j)))
                    if j == 3:
                        if not (last and s + TURN >= STEPS):
                            tb, _, ts = later(b, par, s, TURN)
                            pe_turn_max(pe, tb, ts)
                        if s == 1 and not first:
                            pe_turn_y(pe, b - 1)
                        if s % 2 == 0 and s > 0:
                            pe_turn_out(pe, b, s // 2 - 1)
                        elif s == 0 and not first:
                            pe_turn_out(pe, b - 1, 3)

        def dve_statistics(dve, b):
            for t in range(QT):
                nc.vector.bn_stats(stats[:, t, :], x_all[:, QT * b + t, :]).then_inc(ln_step, 1)
            for t in range(QT):
                dve.wait_ge(ln_step, 7 * b + 1 + t)
                dve.nop(nofuse=True)
                nc.vector.bn_aggr(meanvar[:, t, :], stats[:, t, :]).then_inc(ln_step, 1)
            dve.wait_ge(ln_step, 7 * b + 4)
            nc.vector.tensor_scalar(vareps[:, :], meanvar[:, :, 1], EPS, None, ALU.add).then_inc(ln_step, 1)

        def dve_norm_x(dve, b):
            dve.wait_ge(rooted, b + 1)
            if not (isinstance(b, int) and b == 0):
                dve.wait_ge(front_filled, 7 * (b - 1) + 1)
            for t in range(QT):
                nc.vector.tensor_scalar(xn[:, t, :], x_all[:, QT * b + t, :], meanvar[:, t, 0:1], rstd[:, t:t + 1],
                                        ALU.subtract, ALU.mult).then_inc(ln_step, 1)

        def dve_max(dve, b, s):
            attn, _ = group(s)
            for j in range(GH):
                g = b * STEPS + s
                dve.wait_ge(scored, GH * g + j + 1)
                if j == 0 and not (isinstance(g, int) and g < 4):
                    dve.wait_ge(msplit, 5 * (g - 3))
                a = bank_a[j % 2]
                if attn == 0:
                    nc.vector.tensor_reduce(rowmax[:, s % 4, 0, j:j + 1], a[:, 0:P], AX_X, ALU.max)
                    op = nc.vector.tensor_reduce(rowmax[:, s % 4, 1, j:j + 1], a[:, P:P + T], AX_X, ALU.max)
                else:
                    op = nc.vector.tensor_reduce(rowmax[:, s % 4, :, j], a.rearrange("p (t k) -> p t k", t=QT),
                                                 AX_X, ALU.max)
                op.then_inc(maxed, 1)
                yield

        def dve_front(dve, b, par, item):
            if 1 <= item <= 4:
                n = item - 1
                dve.wait_ge(front_act, 5 * b + 2 + n)
                nc.vector.scalar_tensor_tensor(out=resid[:, n, :], in0=bank_f[:, 0:T], scalar=bqk_sb[:, n:n + 1],
                                               in1=part[:, n, 0, :], op0=ALU.add, op1=ALU.subtract)\
                    .then_inc(front_dve, 1)
                dve.wait_ge(front_dve, 10 * b + 2 * n + 1)
                nc.vector.tensor_copy(part[:, n, 1, :], resid[:, n, :]).then_inc(front_dve, 1)
            elif item in (5, 6):
                dve.wait_ge(front_filled, 7 * b + item + 1)
                if not isinstance(b, int) or b > 1:
                    dve.wait_ge(weighed, STEPS * (b - 1))
                attn = item - 5
                nc.vector.tensor_tensor(
                    vext[:, par, attn, :, :, 0:D],
                    bank_f[:, 0:T].rearrange("p (t h d) -> p t h d", t=QT, d=D),
                    bvp_sb[:, attn, :].rearrange("p (h d) -> p h d", d=D).unsqueeze(1).to_broadcast([P, QT, H, D]),
                    ALU.add).then_inc(front_dve, 1)

        def dve_norm_out(dve, b, r):
            pair = b * 4 + r
            dve.wait_ge(o_turned, pair + 1)
            t = bank_t.rearrange("p (a t j f) -> p a t j f", a=2, t=QT, j=GH)
            nc.vector.reciprocal(rden[:, :, :, :], t[:, :, :, :, D]).then_inc(normed, 1)
            dve.wait_ge(normed, 3 * pair + 1)
            for attn in range(2):
                op = nc.vector.tensor_tensor(ynorm[:, attn], t[:, attn, :, :, 0:D],
                                             rden[:, attn].unsqueeze(3).to_broadcast([P, QT, GH, D]), ALU.mult)
            op.then_inc(normed, 1)
            dve.wait_ge(normed, 3 * pair + 2)
            if r == 0 and not (isinstance(b, int) and b == 0):
                dve.wait_ge(y_turned, b)
            nc.vector.tensor_tensor(y_sb[:, :, QUAD * r:QUAD * (r + 1)].rearrange("p t (j d) -> p t j d", d=D),
                                    ynorm[:, 0], ynorm[:, 1], ALU.add).then_inc(normed, 1)

        def dve_residual(dve, b):
            dve.wait_ge(projected, b + 1)
            nc.vector.tensor_tensor(proj_b[:, :, :], bank_t[:, 0:T].rearrange("p (t c) -> p t c", t=QT),
                                    bvp_sb[:, 2, :].unsqueeze(1).to_broadcast([P, QT, C]), ALU.add)\
                .then_inc(x1_step, 1)
            dve.wait_ge(x1_step, 2 * b + 1)
            for t in range(QT):
                op = nc.vector.scalar_tensor_tensor(out=x_all[:, QT * b + t, :], in0=proj_b[:, t, :],
                                                    scalar=tgate[:, 0:1], in1=x_all[:, QT * b + t, :],
                                                    op0=ALU.mult, op1=ALU.add)
            op.then_inc(x1_step, 1)

        def dve_batch(dve, b, par, first=False, last=False):
            for s in range(STEPS):
                ahead = None
                if not (last and s + LEAD >= STEPS):
                    ab, _, a_s = later(b, par, s, LEAD)
                    ahead = dve_max(dve, ab, a_s)
                for j in range(GH):
                    if ahead:
                        next(ahead)
                    if not last and (s, j) == (0, 0):
                        dve_statistics(dve, b + 1)
                    if not last and (s, j) == (0, 2):
                        dve_norm_x(dve, b + 1)
                    if not last and (s, j) in FRONT_SLOTS:
                        dve_front(dve, b + 1, 1 - par, FRONT_SLOTS.index((s, j)))
                    if j == 0 and s == 2 and not first:
                        dve_residual(dve, b - 1)
                    if j == 3:
                        if s % 2 == 0 and s > 0:
                            dve_norm_out(dve, b, s // 2 - 1)
                        elif s == 0 and not first:
                            dve_norm_out(dve, b - 1, 3)

        def act_exp(act, b, s):
            attn, _ = group(s)
            width = P + T if attn == 0 else 2 * T
            g = b * STEPS + s
            for j in range(GH):
                act.wait_ge(shifted, GH * g + j + 1)
                if j == 0 and not (isinstance(g, int) and g < 2):
                    act.wait_ge(weighed, g - 1)
                nc.scalar.activation(probs[:, GH * (s % 2) + j, 0:width], bank_b[j % 2][:, 0:width], ACT.Exp,
                                     scale=SCALE).then_inc(exped, 1)
                yield

        def act_front(act, b, item):
            if item > 4:
                return
            act.wait_ge(front_filled, 7 * b + item + 1)
            if item == 0:
                nc.scalar.copy(xnT[:, :], bank_f[:, 0:T]).then_inc(front_act, 1)
            else:
                n = item - 1
                if not isinstance(b, int) or b > 0:
                    act.wait_ge(parts_out[n], 16 * b)
                nc.scalar.activation(part[:, n, 0, :], bank_f[:, 0:T], ACT.Identity, bias=bqk_sb[:, n:n + 1])\
                    .then_inc(front_act, 1)

        def act_copy_max(act, b, s):
            g = b * STEPS + s
            act.wait_ge(m_turned, g + 1)
            if not (isinstance(g, int) and g < 2):
                act.wait_ge(m_placed[s % 2], 16 * (b * 4 + s // 2))
            nc.scalar.copy(mrows[:, s % 2, :], bank_m[0:3 * GH, 0:T]).then_inc(m_copied, 1)

        def act_copy_out(act, b, r):
            act.wait_ge(weighed, b * STEPS + 2 * r + 2)
            if not (isinstance(b, int) and b == 0 and r < 2):
                act.wait_ge(o_turned, b * 4 + r - 1)
            nc.scalar.copy(o_sb[:, r % 2, :], bank_o).then_inc(o_copied, 1)

        def act_copy_y(act, b):
            act.wait_ge(y_turned, b + 1)
            nc.scalar.copy(yT[:, :], bank_t[:, 0:T]).then_inc(y_copied, 1)

        def act_weights_high(act, e):
            act.wait_ge(w_staged, 16 * (e + 1))
            nc.scalar.copy(w_hi[:, e, :], w_stage[:, :]).then_inc(w_hi_done, 1)

        def act_batch(act, b, par, first=False, last=False):
            for s in range(STEPS):
                e = act_exp(act, b, s)
                for j in range(GH):
                    next(e)
                    if j == 2:
                        if s % 2 == 0 and s > 0:
                            act_copy_out(act, b, s // 2 - 1)
                        elif s == 0 and not first:
                            act_copy_out(act, b - 1, 3)
                    if j == 3:
                        if not (last and s + TURN >= STEPS):
                            tb, _, ts = later(b, par, s, TURN)
                            act_copy_max(act, tb, ts)
                        if s == 1 and not first:
                            act_copy_y(act, b - 1)
                    if (s, j) == (4, 3):
                        act_weights_high(act, b)
                    if not last and (s, j) in FRONT_SLOTS:
                        act_front(act, b + 1, FRONT_SLOTS.index((s, j)))

        def pool_split_max(pool, b, s):
            g = b * STEPS + s
            n = 5 * g
            mp = mparts[:, s % 2]
            pool.wait_ge(maxed, GH * (g + 1))
            pool.nop(nofuse=True)
            nc.gpsimd.tensor_scalar(negmax[:, :, :], rowmax[:, s % 4], -1.0, None, ALU.mult).then_inc(msplit, 1)
            pool.wait_ge(msplit, n + 1)
            if not (isinstance(g, int) and g < 2):
                pool.wait_ge(m_turned, g - 1)
            pool.nop(nofuse=True)
            nc.gpsimd.tensor_copy(mp[:, :, 0, :], negmax[:, :, :]).then_inc(msplit, 1)
            pool.wait_ge(msplit, n + 2)
            nc.gpsimd.tensor_tensor(negres[:, :, :], negmax[:, :, :], mp[:, :, 0, :], ALU.subtract)\
                .then_inc(msplit, 1)
            pool.wait_ge(msplit, n + 3)
            pool.nop(nofuse=True)
            nc.gpsimd.tensor_copy(mp[:, :, 1, :], negres[:, :, :]).then_inc(msplit, 1)
            pool.wait_ge(msplit, n + 4)
            nc.gpsimd.tensor_tensor(mp[:, :, 2, :], negres[:, :, :], mp[:, :, 1, :], ALU.subtract)\
                .then_inc(msplit, 1)

        def pool_low(pool, b, n):
            pool.wait_ge(front_dve, 10 * b + 2 * n + 2)
            nc.gpsimd.tensor_tensor(part[:, n, 2, :], resid[:, n, :], part[:, n, 1, :], ALU.subtract)\
                .then_inc(low_done, 1)

        def pool_root(pool, b):
            pool.wait_ge(ln_step, 7 * b + 5)
            nc.gpsimd.tensor_tensor(rstd[:, :], vareps[:, :], minus_half[:, 0:QT], ALU.pow).then_inc(rooted, 1)

        def pool_weights_low(pool, e, half):
            pool.wait_ge(w_hi_done, e + 1)
            cols = slice(WCOLS // 2 * half, WCOLS // 2 * (half + 1))
            nc.gpsimd.tensor_tensor(w_lo[:, e, cols], w_stage[:, cols], w_hi[:, e, cols].bitcast(F32), ALU.subtract)\
                .then_inc(w_lo_done, 1)

        def pool_batch(pool, b, par, first=False, last=False):
            for s in range(STEPS):
                if s == 0 and not last:
                    pool_root(pool, b + 1)
                for n in {1: (Q,), 2: (K, QC), 3: (KC,)}.get(s, ()):
                    if not last:
                        pool_low(pool, b + 1, n)
                if not (last and s + LEAD >= STEPS):
                    ab, _, a_s = later(b, par, s, LEAD)
                    pool_split_max(pool, ab, a_s)
                if s in (5, 6):
                    pool_weights_low(pool, b, s - 5)

        def sp_place_max(sp, b, par, s):
            attn, h0 = group(s)
            sp.wait_ge(m_copied, b * STEPS + s + 1)
            sp.dma_start(qstack[ROWS:MROWS, par, attn, h0:h0 + GH, :], mrows[:, s % 2, :])\
                .then_inc(m_placed[s % 2], 16)

        def sp_parts_out(sp, b, n):
            sp.wait_ge(low_done, 4 * b + n + 1)
            if not (isinstance(b, int) and b == 0):
                sp.nop(nofuse=True)
                sp.wait_ge(stacked[n], 16 * (NP if n in (Q, QC) else 1) * b)
            sp.dma_start(scratch[n].rearrange("a p t -> p a t"), part[:, n, :, :]).then_inc(parts_out[n], 16)

        def sp_stack(sp, b, par, n):
            attn = n // 2
            sp.wait_ge(parts_out[n], 16 * (b + 1))
            parts = scratch[n].rearrange("a (d h) t -> a d (h t)", d=D)
            if n in (K, KC):
                sp.dma_start(kstack[0:NP * PART_ROWS, par, attn, :, :].rearrange("p h t -> p (h t)"),
                             parts.unsqueeze(0).to_broadcast([NP, NP, D, H * T])).then_inc(stacked[n], 16)
            else:
                for a in range(NP):
                    rows = slice(PART_ROWS * a, PART_ROWS * (a + 1))
                    sp.dma_start(qstack[rows, par, attn, :, :].rearrange("p h t -> p (h t)"),
                                 parts[a].unsqueeze(0).to_broadcast([NP, D, H * T])).then_inc(stacked[n], 16)

        def sp_batch(sp, b, par, first=False, last=False):
            for s in range(STEPS):
                if s == 0 and not last:
                    if not first:
                        sp.wait_ge(front_filled, 7 * b)
                    sp.nop(nofuse=True)
                    sp.dma_start(ctxT[:, 1 - par, :], ctx_in[b + 1]).then_inc(ctx_loaded[1 - par], 16)
                if s == 2 and not last:
                    sp.wait_ge(shifted, b * STEPS * GH + 1)
                    sp.nop(nofuse=True)
                    sp_parts_out(sp, b + 1, K)
                    sp_stack(sp, b + 1, 1 - par, Q)
                if s == 3 and not last:
                    sp_stack(sp, b + 1, 1 - par, K)
                    sp_parts_out(sp, b + 1, KC)
                    sp_stack(sp, b + 1, 1 - par, QC)
                if s == 4 and not last:
                    sp_stack(sp, b + 1, 1 - par, KC)
                if s == 1:
                    if not first:
                        sp.wait_ge(w_lo_done, 2 * b)
                        sp.nop(nofuse=True)
                    sp.dma_start(w_stage[:, :], w12t[:, b, :]).then_inc(w_staged, 16)
                if not (last and s + TURN >= STEPS):
                    sp_place_max(sp, *later(b, par, s, TURN))
                if s == 1 and not last:
                    sp_parts_out(sp, b + 1, Q)
                if s == 2 and not last:
                    sp_parts_out(sp, b + 1, QC)

        def words(stack, rows, par):
            return stack[rows, par].rearrange("p a h t -> p (a h t)").bitcast(mybir.dt.uint32)

        def stack_zeros(eng, par, done):
            for stack in (qstack, kstack):
                eng.memset(words(stack, slice(64, ROWS), par), 0).then_inc(done, 1)

        def batches(eng, run):
            run(eng, 0, 0, first=True)
            with eng.Fori(0, NB // 2 - 1) as i:
                run(eng, 2 * i + 1, 1)
                run(eng, 2 * i + 2, 0)
            run(eng, NB - 1, 1, last=True)

        with nc.Block() as block:
            @block.sync
            def _(sp):
                sp.dma_start(x_all[:, 0:QT, :], x[:, 0:QT, :]).then_inc(x_in, 16)
                for dst, src in ((wqk_sb[:, :, :], wqk), (bqk_sb[:, :], bqk)):
                    sp.dma_start(dst, src).then_inc(qk_in, 16)
                sp.dma_start(ctxT[:, 0, :], ctx_in[0]).then_inc(ctx_loaded[0], 16)
                for dst, src in ((wck_sb[:, :], wck), (wv_sb[:, :], wv), (wcv_sb[:, :], wcv), (wp_sb[:, :], wp),
                                 (rw_sb[:, :], rwt), (bvp_sb[:, :, :], bvp.unsqueeze(0).to_broadcast([P, 3, C])),
                                 (gate_sb[:, :], gates.unsqueeze(0).to_broadcast([P, 2]))):
                    sp.dma_start(dst, src).then_inc(w_in, 16)
                sp.dma_start(x_all[:, QT:, :], x[:, QT:, :]).then_inc(rest_in, 16)
                sp.wait_ge(const_dve, 1)
                sp.wait_ge(const_pool, 5)
                for n in (Q, K):
                    sp_parts_out(sp, 0, n)
                sp_stack(sp, 0, 0, Q)
                sp_parts_out(sp, 0, QC)
                sp_stack(sp, 0, 0, K)
                sp_parts_out(sp, 0, KC)
                sp_stack(sp, 0, 0, QC)
                sp_stack(sp, 0, 0, KC)
                for s in range(TURN):
                    sp_place_max(sp, 0, 0, s)
                sp.wait_ge(const_pool, 13)
                sp.wait_ge(const_dve, 5)
                batches(sp, sp_batch)

            @block.gpsimd
            def _(pool):
                nc.gpsimd.memset(minus_half[:, :], -0.5).then_inc(const_pool, 1)
                nc.gpsimd.memset(ident[:, :], 0.0).then_inc(const_pool, 1)
                pool.wait_ge(const_pool, 2)
                nc.gpsimd.affine_select(out=ident[:, :], in_=ident[:, :], compare_op=ALU.not_equal, fill=1.0, base=0,
                                        pattern=[[-1, P]], channel_multiplier=1).then_inc(const_pool, 1)
                pool.wait_ge(const_pool, 3)
                stack_zeros(nc.gpsimd, 0, const_pool)
                pool.wait_ge(const_pool, 5)
                pool_root(pool, 0)
                for m in (identb, mask_qk, mask_kq):
                    nc.gpsimd.memset(m[:, :], 0.0).then_inc(const_pool, 1)
                pool.wait_ge(const_pool, 8)
                nc.gpsimd.affine_select(out=identb[:, :], in_=identb[:, :], compare_op=ALU.not_equal, fill=1.0,
                                        base=0, pattern=[[-1, P]], channel_multiplier=1).then_inc(const_pool, 1)
                nc.gpsimd.affine_select(out=mask_qk[:, :], in_=mask_qk[:, :], compare_op=ALU.is_ge, fill=MASKED,
                                        base=0, pattern=[[-1, P]], channel_multiplier=1).then_inc(const_pool, 1)
                nc.gpsimd.affine_select(out=mask_kq[:, :], in_=mask_kq[:, :], compare_op=ALU.is_ge, fill=MASKED,
                                        base=0, pattern=[[1, P]], channel_multiplier=-1).then_inc(const_pool, 1)
                pool.wait_ge(const_pool, 11)
                stack_zeros(nc.gpsimd, 1, const_pool)
                pool.wait_ge(const_pool, 13)
                for i in range(4):
                    pool_low(pool, 0, i)
                for s in range(LEAD):
                    pool_split_max(pool, 0, s)
                batches(pool, pool_batch)

            @block.scalar
            def _(act):
                act.wait_ge(qk_in, 32)
                for item in range(5):
                    act_front(act, 0, item)
                act.wait_ge(w_in, 16 * 7)
                nc.scalar.activation(tgate[:, :], gate_sb[:, :], ACT.Tanh).then_inc(gate_done, 1)
                for s in range(TURN):
                    act_copy_max(act, 0, s)
                batches(act, act_batch)
                act_copy_out(act, NB - 1, 3)
                act_copy_y(act, NB - 1)

            @block.vector
            def _(dve):
                nc.vector.memset(words(kstack, slice(ROWS, MROWS), 0), BF16_ONES).then_inc(const_dve, 1)
                dve.wait_ge(x_in, 16)
                dve_statistics(dve, 0)
                dve_norm_x(dve, 0)
                nc.vector.memset(vext[:, :, :, :, :, D:D + 1], 1.0).then_inc(const_dve, 1)
                nc.vector.memset(vext[:, :, :, :, :, D + 1:], 0.0).then_inc(const_dve, 1)
                dve.wait_ge(qk_in, 32)
                for item in range(5):
                    dve_front(dve, 0, 0, item)
                dve.wait_ge(w_in, 16 * 7)
                for item in (5, 6):
                    dve_front(dve, 0, 0, item)
                nc.vector.memset(vext[:, 1, :, :, :, 0:D], 0.0).then_inc(const_dve, 1)
                nc.vector.memset(words(kstack, slice(ROWS, MROWS), 1), BF16_ONES).then_inc(const_dve, 1)
                dve.wait_ge(rest_in, 16)
                dve.wait_ge(gate_done, 1)
                for s in range(LEAD):
                    for _step in dve_max(dve, 0, s):
                        pass
                batches(dve, dve_batch)
                dve_norm_out(dve, NB - 1, 3)
                dve_residual(dve, NB - 1)

            @block.tensor
            def _(pe):
                pe.wait_ge(const_pool, 3)
                pe_front(pe, 0, 0, 0)
                pe.wait_ge(qk_in, 32)
                for item in range(1, 4):
                    pe_front(pe, 0, 0, item)
                pe.wait_ge(w_in, 16 * 7)
                for item in range(4, 7):
                    pe_front(pe, 0, 0, item)
                pe.wait_ge(const_pool, 11)
                pe.wait_ge(const_dve, 5)
                for s in range(LEAD):
                    for _step in pe_scores(pe, 0, 0, s):
                        pass
                    if s > 0:
                        pe_turn_max(pe, 0, s - 1)
                batches(pe, pe_batch)
                for _half in pe_weigh(pe, NB - 1, 1, STEPS - 1):
                    pass
                pe_turn_out(pe, NB - 1, 3)
                pe_turn_y(pe, NB - 1)
                pe_project(pe, NB - 1)

        attention.close()
        experts(nc, es, x_all, tgate, ident, identb, w_hi, w_lo, rw_sb,
                minus_half, psum, out)


def experts(nc, es, x_all, tgate, ident, identb, w_hi, w_lo, rw_sb, minus_half,
            psum, out):
    def sb(name, shape, dt=F32):
        return es.enter_context(nc.sbuf_tensor(name, shape, dt))

    def sem(name):
        return es.enter_context(nc.semaphore(name))

    NTOK = NB * T
    xn2 = sb("xn2", [P, CT, C])
    stats2 = sb("stats2", [P, CT, 6])
    meanvar2 = sb("meanvar2", [P, CT, 2])
    vareps2 = sb("vareps2", [P, CT])
    rstd2 = sb("rstd2", [P, CT])
    x_t = sb("x_t", [P, CHUNK])
    x_hi = sb("x_hi", [P, NTOK], F32R)
    x_lo = sb("x_lo", [P, NTOK], F32R)
    logit = sb("logit", [P, CT, NE])
    top = sb("top", [P, CT])
    total = sb("total", [P, CT])
    expo = sb("expo", [P, CT, NE])
    prob = sb("prob", [P, CT, NE])
    earlier = sb("earlier", [P, NE, NE])
    above = sb("above", [P, CT, NE, NE])
    ties = sb("ties", [P, CT, NE, NE])
    rank = sb("rank", [P, CT, NE])
    comb = sb("comb", [P, CT, NE])
    combres = sb("combres", [P, CT, NE])
    combparts = sb("combparts", [P, CT, 3, NE], BF16)
    comb_t = sb("comb_t", [3 * NE, NTOK], BF16)
    pick = sb("pick", [3 * NE, NE, P], BF16)
    silu = sb("silu", [P, IT, CHUNK])
    gated = sb("gated", [P, IT, CHUNK])
    y = sb("y", [P, 2, IT, CHUNK])
    y_hi = sb("y_hi", [P, 2, IT, CHUNK], F32R)
    y_lo = sb("y_lo", [P, 2, IT, CHUNK], F32R)
    out_t = sb("out_t", [P, CHUNK])

    bank_gate = [psum[:, k, :] for k in range(IT)]
    bank_up = [psum[:, IT + k, :] for k in range(IT)]
    bank_comb = [psum[:, 4, :], psum[:, 7, :]]
    bank_out = psum[:, 5, :]
    bank_turn = psum[:, 6, :]

    consts = sem("consts")
    norm_step, rooted2 = sem("norm_step"), sem("rooted2")
    x_turned, x_rounded, x_copied, x_split = sem("x_turned"), sem("x_rounded"), sem("x_copied"), sem("x_split")
    routed, shifted_logits, expo_done, route_step = sem("routed"), sem("shifted_logits"), sem("expo_done"), sem("route_step")
    comb_step, comb_turned, comb_copied = sem("comb_step"), sem("comb_turned"), sem("comb_copied")
    comb_spread = sem("comb_spread")
    gate_ready, gate_read = sem("gate_ready"), sem("gate_read")
    up_ready, up_read = sem("up_ready"), sem("up_read")
    y_ready, y_rounded, y_split = sem("y_ready"), sem("y_rounded"), sem("y_split")
    gated_done = sem("gated_done")
    down_done = sem("down_done")
    out_ready, out_copied, out_turned, out_added, stored = (
        sem("out_ready"), sem("out_copied"), sem("out_turned"), sem("out_added"), sem("stored"))
    ROUTE = 12
    NORM = 2 * CT + 1 + CT

    def chunks(eng, run):
        run(eng, 0, first=True)
        with eng.Fori(1, NCHUNK - 1) as c:
            run(eng, c)
        run(eng, NCHUNK - 1, last=True)

    with nc.Block() as block:
        @block.gpsimd
        def _(pool):
            nc.gpsimd.memset(pick[:, :, :], 0.0).then_inc(consts, 1)
            pool.wait_ge(consts, 1)
            for c in range(3):
                nc.gpsimd.affine_select(out=pick[:, :, :], in_=pick[:, :, :], compare_op=ALU.not_equal, fill=1.0,
                                        base=-NE * c, pattern=[[-1, NE], [0, P]], channel_multiplier=1)\
                    .then_inc(consts, 1)
                pool.wait_ge(consts, 2 + c)
            nc.gpsimd.memset(earlier[:, :, :], 1.0).then_inc(consts, 1)
            pool.wait_ge(consts, 5)
            nc.gpsimd.affine_select(out=earlier[:, :, :], in_=earlier[:, :, :], compare_op=ALU.is_ge, fill=0.0,
                                    base=-1, pattern=[[1, NE], [-1, NE]], channel_multiplier=0).then_inc(consts, 1)
            def pool_root(pc):
                pool.wait_ge(norm_step, NORM * pc + 2 * CT + 1)
                nc.gpsimd.tensor_tensor(rstd2[:, :], vareps2[:, :], minus_half[:, :], ALU.pow).then_inc(rooted2, 1)

            def pool_split_x(pc):
                pool.wait_ge(x_rounded, pc + 1)
                pool.wait_ge(x_copied, pc + 1)
                nc.gpsimd.tensor_tensor(x_lo[:, bass.ds(pc * CHUNK, CHUNK)], x_t[:, :],
                                        x_hi[:, bass.ds(pc * CHUNK, CHUNK)].bitcast(F32), ALU.subtract)\
                    .then_inc(x_split, 1)

            def pool_chunk(_, c, first=False, last=False):
                for e in range(NE):
                    for k in range(IT):
                        n = (c * NE + e) * IT + k
                        pool.wait_ge(y_rounded, n + 1)
                        pool.wait_ge(down_done, n + 1)
                        nc.gpsimd.tensor_tensor(y_lo[:, e % 2, k, :], y[:, e % 2, k, :],
                                                y_hi[:, e % 2, k, :].bitcast(F32), ALU.subtract).then_inc(y_split, 1)
                        if not last and (e, k) == (0, 1):
                            pool_root(c + 1)
                        if not last and (e, k) == (3, 1):
                            pool_split_x(c + 1)

            pool_root(0)
            pool_split_x(0)
            pool.nop().then_inc(y_split, 4)
            chunks(pool, pool_chunk)

        @block.scalar
        def _(act):
            def act_round_x(pc):
                act.wait_ge(x_turned, pc + 1)
                nc.scalar.copy(x_hi[:, bass.ds(pc * CHUNK, CHUNK)], bank_turn).then_inc(x_rounded, 1)

            def act_exp_logits(pc):
                act.wait_ge(shifted_logits, pc + 1)
                nc.scalar.activation(expo[:, :, :], logit[:, :, :], ACT.Exp).then_inc(expo_done, 1)

            def act_copy_out(c):
                act.wait_ge(out_ready, c + 1)
                act.wait_ge(out_turned, c + 1)
                nc.scalar.copy(out_t[:, :], bank_out).then_inc(out_copied, 1)

            def act_chunk(_, c, first=False, last=False):
                def round_y(e, k):
                    n = (c * NE + e) * IT + k
                    act.wait_ge(y_ready, n + 1)
                    act.wait_ge(down_done, n + 1)
                    nc.scalar.copy(y_hi[:, e % 2, k, :], y[:, e % 2, k, :]).then_inc(y_rounded, 1)

                for e in range(NE):
                    for k in range(IT):
                        n = (c * NE + e) * IT + k
                        act.wait_ge(gate_ready, n + 1)
                        act.wait_ge(up_read, n + 1)
                        nc.scalar.activation(silu[:, k, :], bank_gate[k], ACT.Silu).then_inc(gate_read, 1)
                        if k == 1:
                            round_y(e, 0)
                        elif e > 0:
                            round_y(e - 1, 1)
                        if (e, k) == (1, 0) and not first:
                            act_copy_out(c - 1)
                        if not last and (e, k) == (3, 0):
                            act_round_x(c + 1)
                        if not last and (e, k) == (4, 0):
                            act_exp_logits(c + 1)
                round_y(NE - 1, 1)

            act_round_x(0)
            act_exp_logits(0)
            act.nop().then_inc(gate_read, 2)
            act.nop().then_inc(out_copied, 1)
            chunks(act, act_chunk)
            act_copy_out(NCHUNK - 1)

        @block.vector
        def _(dve):
            def norm(pc, piece):
                if piece == 0:
                    for t in range(CT):
                        nc.vector.bn_stats(stats2[:, t, :], x_all[:, CT * pc + t, :]).then_inc(norm_step, 1)
                elif piece == 1:
                    dve.wait_ge(norm_step, NORM * pc + CT)
                    dve.nop(nofuse=True)
                    for t in range(CT):
                        nc.vector.bn_aggr(meanvar2[:, t, :], stats2[:, t, :]).then_inc(norm_step, 1)
                    dve.wait_ge(norm_step, NORM * pc + 2 * CT)
                    nc.vector.tensor_scalar(vareps2[:, :], meanvar2[:, :, 1], EPS, None, ALU.add)\
                        .then_inc(norm_step, 1)
                else:
                    if piece == 2:
                        dve.wait_ge(rooted2, pc + 1)
                        if not isinstance(pc, int) or pc > 0:
                            dve.wait_ge(x_turned, pc)
                    for t in range(2 * piece - 4, 2 * piece - 2):
                        nc.vector.tensor_scalar(xn2[:, t, :], x_all[:, CT * pc + t, :], meanvar2[:, t, 0:1],
                                                rstd2[:, t:t + 1], ALU.subtract, ALU.mult).then_inc(norm_step, 1)

            def copy_x(pc):
                dve.wait_ge(x_rounded, pc + 1)
                if not isinstance(pc, int) or pc > 0:
                    dve.wait_ge(routed, pc)
                    dve.wait_ge(x_split, pc)
                nc.vector.tensor_copy(x_t[:, :], bank_turn).then_inc(x_copied, 1)

            def route(pc, piece):
                step = ROUTE * pc
                r = bank_turn[:, 0:CT * NE].rearrange("p (t e) -> p t e", e=NE)
                other = prob[:, :, :].unsqueeze(2).to_broadcast([P, CT, NE, NE])
                own = prob[:, :, :].unsqueeze(3).to_broadcast([P, CT, NE, NE])
                if piece == 0:
                    dve.wait_ge(routed, pc + 1)
                    nc.vector.tensor_reduce(top[:, :], r, AX_X, ALU.max).then_inc(route_step, 1)
                    dve.wait_ge(route_step, step + 1)
                    nc.vector.tensor_tensor(logit[:, :, :], r, top[:, :].unsqueeze(2).to_broadcast([P, CT, NE]),
                                            ALU.subtract).then_inc(shifted_logits, 1)
                elif piece == 1:
                    dve.wait_ge(expo_done, pc + 1)
                    nc.vector.tensor_reduce(top[:, :], expo[:, :, :], AX_X, ALU.add).then_inc(route_step, 1)
                    dve.wait_ge(route_step, step + 2)
                    nc.vector.reciprocal(total[:, :], top[:, :]).then_inc(route_step, 1)
                    dve.wait_ge(route_step, step + 3)
                    nc.vector.tensor_tensor(prob[:, :, :], expo[:, :, :],
                                            total[:, :].unsqueeze(2).to_broadcast([P, CT, NE]), ALU.mult)\
                        .then_inc(route_step, 1)
                elif piece == 2:
                    dve.wait_ge(route_step, step + 4)
                    nc.vector.tensor_tensor(above[:, :, :, :], other, own, ALU.is_gt).then_inc(route_step, 1)
                    nc.vector.tensor_tensor(ties[:, :, :, :], other, own, ALU.is_ge).then_inc(route_step, 1)
                    dve.wait_ge(route_step, step + 6)
                    nc.vector.tensor_tensor(ties[:, :, :, :], ties[:, :, :, :],
                                            earlier[:, :, :].unsqueeze(1).to_broadcast([P, CT, NE, NE]), ALU.mult)\
                        .then_inc(route_step, 1)
                elif piece == 3:
                    dve.wait_ge(route_step, step + 7)
                    nc.vector.tensor_tensor(above[:, :, :, :], above[:, :, :, :], ties[:, :, :, :], ALU.max)\
                        .then_inc(route_step, 1)
                    dve.wait_ge(route_step, step + 8)
                    nc.vector.tensor_reduce(rank[:, :, :], above[:, :, :, :], AX_X, ALU.add).then_inc(route_step, 1)
                    dve.wait_ge(route_step, step + 9)
                    nc.vector.scalar_tensor_tensor(out=comb[:, :, :], in0=rank[:, :, :], scalar=float(TOPK),
                                                   in1=prob[:, :, :], op0=ALU.is_lt, op1=ALU.mult)\
                        .then_inc(route_step, 1)
                elif piece == 4:
                    dve.wait_ge(route_step, step + 10)
                    if not isinstance(pc, int) or pc > 0:
                        dve.wait_ge(comb_turned, pc)
                    nc.vector.tensor_copy(combparts[:, :, 0, :], comb[:, :, :]).then_inc(route_step, 1)
                    dve.wait_ge(route_step, step + 11)
                    nc.vector.tensor_tensor(combres[:, :, :], comb[:, :, :], combparts[:, :, 0, :], ALU.subtract)\
                        .then_inc(route_step, 1)
                    dve.wait_ge(route_step, step + 12)
                    nc.vector.tensor_copy(combparts[:, :, 1, :], combres[:, :, :]).then_inc(comb_step, 1)
                    dve.wait_ge(comb_step, 2 * pc + 1)
                    nc.vector.tensor_tensor(combparts[:, :, 2, :], combres[:, :, :], combparts[:, :, 1, :],
                                            ALU.subtract).then_inc(comb_step, 1)
                else:
                    dve.wait_ge(comb_turned, pc + 1)
                    nc.vector.tensor_copy(comb_t[:, bass.ds(pc * CHUNK, CHUNK)],
                                          bank_turn.bitcast(BF16)[0:3 * NE, 0:CHUNK]).then_inc(comb_copied, 1)

            def add_out(c):
                dve.wait_ge(out_turned, c + 2)
                for t in range(CT):
                    op = nc.vector.scalar_tensor_tensor(out=x_all[:, CT * c + t, :],
                                                        in0=bank_turn[:, P * t:P * (t + 1)],
                                                        scalar=tgate[:, 1:2], in1=x_all[:, CT * c + t, :],
                                                        op0=ALU.mult, op1=ALU.add)
                op.then_inc(out_added, 1)

            PREPARE = {(0, 0): (norm, 0), (0, 1): (norm, 1), (1, 0): (norm, 2), (1, 1): (norm, 3),
                       (3, 0): (copy_x,), (4, 0): (route, 0), (5, 0): (route, 1), (5, 1): (route, 2),
                       (6, 0): (route, 3), (6, 1): (route, 4), (7, 0): (route, 5)}

            def dve_chunk(_, c, first=False, last=False):
                for e in range(NE):
                    for k in range(IT):
                        n = (c * NE + e) * IT + k
                        dve.wait_ge(up_ready, n + 1)
                        dve.wait_ge(gate_read, n + 3)
                        nc.vector.tensor_tensor(gated[:, k, :], silu[:, k, :], bank_up[k], ALU.mult)\
                            .then_inc(up_read, 1)
                        dve.wait_ge(up_read, n + 3)
                        dve.wait_ge(comb_spread, c * NE + e + 1)
                        dve.wait_ge(y_split, n + 1)
                        nc.vector.tensor_tensor(y[:, e % 2, k, :], gated[:, k, :], bank_comb[e % 2], ALU.mult)\
                            .then_inc(y_ready, 1)
                        if (e, k) == (2, 0) and not first:
                            add_out(c - 1)
                        if not last and (e, k) in PREPARE:
                            step, *piece = PREPARE[e, k]
                            step(c + 1, *piece)

            dve.nop().then_inc(up_read, 2)
            for piece in range(4):
                norm(0, piece)
            copy_x(0)
            dve.wait_ge(consts, 6)
            for piece in range(6):
                route(0, piece)
            dve.nop().then_inc(out_added, 1)
            chunks(dve, dve_chunk)
            add_out(NCHUNK - 1)

        @block.tensor
        def _(pe):
            def turn_x(pc):
                pe.wait_ge(norm_step, NORM * (pc + 1))
                if not isinstance(pc, int) or pc > 0:
                    pe.wait_ge(out_added, pc)
                    pe.wait_ge(comb_copied, pc)
                for t in range(CT):
                    mm = nc.tensor.transpose(bank_turn[:, P * t:P * (t + 1)], xn2[:, t, :], ident[:, :])
                mm.then_inc(x_turned, 1)

            def route(pc):
                pe.wait_ge(x_copied, pc + 1)
                for t in range(CT):
                    mm = nc.tensor.matmul(bank_turn[:, NE * t:NE * (t + 1)], x_t[:, P * t:P * (t + 1)], rw_sb[:, :],
                                          start=True, stop=True)
                mm.then_inc(routed, 1)

            def turn_comb(pc):
                pe.wait_ge(comb_step, 2 * pc + 2)
                pe.nop(nofuse=True)
                for t in range(CT):
                    mm = nc.tensor.transpose(bank_turn.bitcast(BF16)[0:3 * NE, P * t:P * (t + 1)],
                                             combparts[:, t, :, :].rearrange("p c e -> p (c e)"), identb[:, :])
                mm.then_inc(comb_turned, 1)

            def turn_out(c):
                pe.wait_ge(out_copied, c + 2)
                if not isinstance(c, int) or c < NCHUNK - 1:
                    pe.wait_ge(comb_copied, c + 2)
                for t in range(CT):
                    mm = nc.tensor.transpose(bank_turn[:, P * t:P * (t + 1)], out_t[:, P * t:P * (t + 1)], ident[:, :])
                mm.then_inc(out_turned, 1)

            def down(c, e, k):
                n = (c * NE + e) * IT + k
                pe.wait_ge(y_split, n + 5)
                if e == 0 and k == 0:
                    pe.wait_ge(out_copied, c + 1)
                col = 2 * INTER + C * k
                for i, (w, yy) in enumerate(((w_hi, y_hi), (w_hi, y_lo), (w_lo, y_hi))):
                    mm = nc.tensor.matmul(bank_out, w[:, e, col:col + C], yy[:, e % 2, k, :],
                                          start=e + k + i == 0, stop=e == NE - 1 and k == IT - 1 and i == 2)
                mm.then_inc(down_done, 1)
                if e == NE - 1 and k == IT - 1:
                    pe.wait_ge(down_done, n + 5)
                    pe.sem_inc(out_ready, 1)

            def pe_chunk(_, c, first=False, last=False):
                tok = bass.ds(c * CHUNK, CHUNK)
                pe.wait_ge(x_split, c + 1)

                def up(e, k):
                    n = (c * NE + e) * IT + k
                    for bank, col, read, ready in ((bank_gate[k], P * k, gate_read, gate_ready),
                                                   (bank_up[k], INTER + P * k, up_read, up_ready)):
                        pe.wait_ge(read, n + 1)
                        for i, (w, xx) in enumerate(((w_hi, x_hi), (w_hi, x_lo), (w_lo, x_hi))):
                            mm = nc.tensor.matmul(bank, w[:, e, col:col + P], xx[:, tok], start=i == 0, stop=i == 2)
                        mm.then_inc(ready, 1)

                for e in range(NE):
                    for k in range(IT):
                        up(e, k)
                        if k == 0:
                            if first and e == 0:
                                turn_comb(0)
                            if e == 0:
                                pe.wait_ge(comb_copied, c + 1)
                            if not (first and e < 2):
                                pe.wait_ge(y_ready, (c * NE + e - 1) * IT)
                            pe.nop(nofuse=True)
                            nc.tensor.matmul(bank_comb[e % 2], pick[:, e, :], comb_t[:, tok], start=True, stop=True)\
                                .then_inc(comb_spread, 1)
                        if e > 0:
                            down(c, e - 1, k)
                        elif not first:
                            down(c - 1, NE - 1, k)
                        if (e, k) == (1, 1) and not first:
                            turn_out(c - 1)
                        if not last:
                            if (e, k) == (2, 1):
                                turn_x(c + 1)
                            if (e, k) == (3, 1):
                                route(c + 1)
                            if (e, k) == (7, 0):
                                turn_comb(c + 1)

            turn_x(0)
            route(0)
            pe.nop().then_inc(down_done, 4)
            pe.nop().then_inc(out_turned, 1)
            chunks(pe, pe_chunk)
            for k in range(IT):
                down(NCHUNK - 1, NE - 1, k)
            turn_out(NCHUNK - 1)

        @block.sync
        def _(sp):
            with sp.Fori(0, NCHUNK) as c:
                sp.wait_ge(out_added, c + 2)
                sp.nop(nofuse=True)
                sp.dma_start(out[:, bass.ds(c * CT, CT), :], x_all[:, bass.ds(c * CT, CT), :]).then_inc(stored, 16)
            sp.wait_ge(stored, 16 * NCHUNK)


def kernel(**inputs):
    import numpy as np
    from concourse import bacc
    from concourse.bass_utils import run_bass_kernel_spmd

    def a(name):
        return np.asarray(inputs[name])

    def turned(w):
        return np.ascontiguousarray(w.reshape(*w.shape[:-1], H, D).swapaxes(-1, -2).reshape(w.shape))

    x = "L0_xattn_"
    arrays = {
        "x": np.ascontiguousarray(a("x").reshape(NTILE, P, C).transpose(1, 0, 2)),
        "ctx_in": np.ascontiguousarray(a("ctx_512").transpose(0, 2, 1)),
        "gates": np.concatenate([a("g_xattn"), a("g_ffn")]),
        "wqk": np.ascontiguousarray(np.stack([turned(a(x + n)) for n in ("Wq", "Wk", "Wcq")], 1)),
        "wck": turned(a(x + "Wck")),
        "bqk": np.ascontiguousarray(np.stack([turned(a(x + n)) for n in ("bq", "bk", "bcq", "bck")], 1)),
        "wv": a(x + "Wv"), "wcv": a(x + "Wcv"), "wp": a(x + "Wp"),
        "bvp": np.stack([a(x + n) for n in ("bv", "bcv", "bp")]),
        "w12t": np.concatenate([
            a("L0_ffn_w1").transpose(2, 0, 1),
            a("L0_ffn_w2").reshape(NE, C, IT, P).transpose(3, 0, 2, 1).reshape(P, NE, IT * C)], 2),
        "rwt": np.ascontiguousarray(a("L0_ffn_router_w").T),
    }
    nc = bacc.Bacc("TRN2", target_bir_lowering=False, num_devices=1)
    args = {n: nc.dram_tensor(n, v.shape, mybir.dt.from_np(v.dtype), kind="ExternalInput").ap()
            for n, v in arrays.items()}
    args["scratch"] = [nc.dram_tensor(f"parts{n}", (NP, P, T), BF16, kind="Internal").ap() for n in range(4)]
    args["out"] = nc.dram_tensor("out", (P, NTILE, C), F32, kind="ExternalOutput").ap()
    gated_attention_experts(nc, **args)
    r = run_bass_kernel_spmd(nc, [arrays], core_ids=[0])
    return r.results[0]["out"].transpose(1, 0, 2).reshape(NB, T, C)
```

```python
from contextlib import ExitStack

import concourse.bass as bass
from concourse import mybir

F32 = mybir.dt.float32
F32R = mybir.dt.float32r
BF16 = mybir.dt.bfloat16
ALU = mybir.AluOpType
ACT = mybir.ActivationFunctionType
AX_X = mybir.AxisListType.X

P = 128
NB, T, C = 8, 256, 128
CC = 64
H, D = 16, 8
QT = T // P
NTILE = NB * QT
STEPS = 8
GH = 4
QUAD = P // GH
SCALE = float(D) ** -0.5
MASKED = -1e30
BF16_ONES = 0x3F803F80
EPS = 1e-5
NP = 3
PART_ROWS = NP * D
ROWS = 96
MROWS = ROWS + 3
Q, K, QC, KC = range(4)
NE, INTER, TOPK = 8, 256, 2
CHUNK = 512
NTOK = NB * T
NCHUNK = NTOK // CHUNK
CT = CHUNK // P
IT = INTER // P
WCOLS = 2 * INTER + IT * C


def gated_attention_experts(nc, x, ctx_in, gates, wqk, wck, bqk, wv, wcv, wp, bvp, w12t, rwt, ones_in, scratch, out):
    with ExitStack() as es, ExitStack() as stacks:
        def kept(name, shape, dt=F32):
            return es.enter_context(nc.sbuf_tensor(name, shape, dt))

        def sb(name, shape, dt=F32):
            return es.enter_context(nc.sbuf_tensor(name, shape, dt))

        def stack_sb(name, shape, dt):
            return stacks.enter_context(nc.sbuf_tensor(name, shape, dt))

        def sem(name):
            return es.enter_context(nc.semaphore(name))

        x_all = kept("x_all", [P, NTILE, C])
        tgate = kept("tgate", [P, 2])
        ident = kept("ident", [P, P])
        identb = kept("identb", [P, P], BF16)
        minus_half = kept("minus_half", [P, CT])
        w_hi = kept("w_hi", [P, NE, WCOLS], F32R)
        w_lo = kept("w_lo", [P, NE, WCOLS], F32R)
        rw_sb = kept("rw_sb", [P, NE])
        w_stage = sb("w_stage", [P, WCOLS])
        wqk_sb = sb("wqk_sb", [P, 3, C])
        wck_sb = sb("wck_sb", [CC, C])
        bqk_sb = sb("bqk_sb", [P, 4])
        wv_sb = sb("wv_sb", [P, C])
        wcv_sb = sb("wcv_sb", [CC, C])
        wp_sb = sb("wp_sb", [P, C])
        bvp_sb = sb("bvp_sb", [P, 3, C])
        gate_sb = sb("gate_sb", [P, 2])
        mask_qk = sb("mask_qk", [P, P], BF16)
        vext = sb("vext", [P, 2, 2, QT, H, QUAD])
        xn = sb("xn", [P, QT, C])
        xnT = sb("xnT", [P, T])
        ctxT = sb("ctxT", [CC, 2, T])
        stats = sb("stats", [P, QT, 6])
        meanvar = sb("meanvar", [P, QT, 2])
        vareps = sb("vareps", [P, QT])
        rstd = sb("rstd", [P, QT])
        part = sb("part", [P, 4, 3, T], BF16)
        resid = sb("resid", [P, 4, T])
        rowmax = sb("rowmax", [P, 4, QT, GH])
        negmax = sb("negmax", [P, QT, GH])
        negres = sb("negres", [P, QT, GH])
        mparts = sb("mparts", [P, 2, QT, 3, GH], BF16)
        mrows = sb("mrows", [3 * GH, 2, T], BF16)
        probs = sb("probs", [P, 2 * GH, 2 * T])
        o_sb = sb("o_sb", [P, 2, 2 * T])
        rden = sb("rden", [P, 2, QT, GH])
        ynorm = sb("ynorm", [P, 2, QT, GH, D])
        y_sb = sb("y_sb", [P, QT, C])
        yT = sb("yT", [P, T])
        proj_b = sb("proj_b", [P, QT, C])

        qstack, kstack = [], []
        for par in range(2):
            qstack.append(stack_sb(f"qstack{par}", [MROWS, 2, H, T], BF16))
            kstack.append(stack_sb(f"kstack{par}", [MROWS, 2, H, T], BF16))
        stacks.close()

        xn2 = sb("xn2", [P, CT, C])
        stats2 = sb("stats2", [P, CT, 6])
        meanvar2 = sb("meanvar2", [P, CT, 2])
        vareps2 = sb("vareps2", [P, CT])
        rstd2 = sb("rstd2", [P, CT])
        x_t = sb("x_t", [P, CHUNK])
        x_hi = sb("x_hi", [P, NTOK], F32R)
        x_lo = sb("x_lo", [P, NTOK], F32R)
        logit = sb("logit", [P, CT, NE])
        top = sb("top", [P, CT])
        total = sb("total", [P, CT])
        silu_neg = sb("silu_neg", [P, CT, NE])
        silu_pos = sb("silu_pos", [P, CT, NE])
        expo = sb("expo", [P, CT, NE])
        prob = sb("prob", [P, CT, NE])
        earlier = sb("earlier", [P, NE, NE])
        above = sb("above", [P, CT, NE, NE])
        ties = sb("ties", [P, CT, NE, NE])
        rank = sb("rank", [P, CT, NE])
        comb = sb("comb", [P, CT, NE])
        combres = sb("combres", [P, CT, NE])
        combparts = sb("combparts", [P, CT, 3, NE], BF16)
        comb_t = sb("comb_t", [3 * NE, NTOK], BF16)
        pick = sb("pick", [3 * NE, NE, P], BF16)
        silu = sb("silu", [P, IT, CHUNK])
        gated = sb("gated", [P, IT, CHUNK])
        y = sb("y", [P, 2, IT, CHUNK])
        y_hi = sb("y_hi", [P, 2, IT, CHUNK], F32R)
        y_lo = sb("y_lo", [P, 2, IT, CHUNK], F32R)
        out_t = sb("out_t", [P, CHUNK])

        psum = es.enter_context(nc.psum_tensor("psum", [P, 8, 512], F32))
        bank_a = [psum[:, 0, :], psum[:, 1, :]]
        bank_b = [psum[:, 2, :], psum[:, 3, :]]
        bank_o = psum[:, 4, :]
        bank_t = psum[:, 5, :]
        bank_f = psum[:, 6, :]
        bank_m = psum[:, 7, :].bitcast(BF16)

        bank_gate = [psum[:, k, :] for k in range(IT)]
        bank_up = [psum[:, IT + k, :] for k in range(IT)]
        bank_comb = [psum[:, 7, :], psum[:, 4, :]]
        bank_out = psum[:, 5, :]
        bank_turn = psum[:, 6, :]

        x_in, qk_in, w_in, rest_in = sem("x_in"), sem("qk_in"), sem("w_in"), sem("rest_in")
        ctx_loaded = [sem("ctx_loaded0"), sem("ctx_loaded1")]
        gate_in = sem("gate_in")
        ones_placed = sem("ones_placed")
        const_pool, const_dve = sem("const_pool"), sem("const_dve")
        gate_done = sem("gate_done")
        ln_step = sem("ln_step")
        rooted = sem("rooted")
        front_filled = sem("front_filled")
        front_act = sem("front_act")
        front_dve = sem("front_dve")
        front_mid = sem("front_mid")
        x_normed = sem("x_normed")
        low_done = sem("low_done")
        parts_out = [sem(f"parts_out{n}") for n in range(4)]
        stacked = [sem(f"stacked{n}") for n in range(4)]
        scored = sem("scored")
        maxed = sem("maxed")
        msplit = sem("msplit")
        m_turned = sem("m_turned")
        m_copied = sem("m_copied")
        m_placed = [sem("m_placed0"), sem("m_placed1")]
        shifted = sem("shifted")
        exped = sem("exped")
        cleared = sem("cleared")
        weighed = sem("weighed")
        o_copied = sem("o_copied")
        o_turned = sem("o_turned")
        normed = sem("normed")
        y_turned, y_copied, projected = sem("y_turned"), sem("y_copied"), sem("projected")
        x1_step = sem("x1_step")
        w_staged = sem("w_staged")
        w_hi_done = sem("w_hi_done")
        w_lo_done = sem("w_lo_done")

        consts = sem("consts")
        norm_step, rooted2 = sem("norm_step"), sem("rooted2")
        x_turned, x_rounded, x_copied, x_split = sem("x_turned"), sem("x_rounded"), sem("x_copied"), sem("x_split")
        routed, shifted_logits, expo_done, route_step = sem("routed"), sem("shifted_logits"), sem("expo_done"), sem("route_step")
        comb_step, comb_turned, comb_copied = sem("comb_step"), sem("comb_turned"), sem("comb_copied")
        comb_spread, divided = sem("comb_spread"), sem("divided")
        gate_ready, gate_read = sem("gate_ready"), sem("gate_read")
        up_ready, up_read = sem("up_ready"), sem("up_read")
        y_ready, y_rounded, y_split = sem("y_ready"), sem("y_rounded"), sem("y_split")
        gated_done = sem("gated_done")
        down_done = sem("down_done")
        out_copied, out_turned, out_added, stored = (
            sem("out_copied"), sem("out_turned"), sem("out_added"), sem("stored"))
        ROUTE = 12
        NORM = 2 * CT + 1 + CT

        def group(s):
            return s % 2, GH * (s // 2)

        LEAD, TURN = 3, 2
        FRONT_SLOTS = [(1, 0), (1, 1), (1, 3), (2, 1), (2, 3), (3, 1), (3, 3)]

        def tail_bank(b, r=3):
            return bank_turn if isinstance(b, int) and b == NB - 1 and r == 3 else bank_t

        def front_bank(b, item):
            if isinstance(b, int) and b == 0:
                return [bank_f, bank_f, bank_o, bank_t, bank_a[0], bank_a[1], bank_b[0]][item]
            return bank_f

        def pe_turn_x(pe, pc):
            pe.wait_ge(norm_step, NORM * (pc + 1))
            if not isinstance(pc, int) or pc == 1:
                pe.wait_ge(x1_step, 2 * NB)
            if not isinstance(pc, int) or pc > 0:
                pe.wait_ge(out_added, pc)
                pe.wait_ge(comb_copied, pc)
            for t in range(CT):
                mm = nc.tensor.transpose(bank_turn[:, P * t:P * (t + 1)], xn2[:, t, :], ident[:, :])
            mm.then_inc(x_turned, 1)

        def pe_route(pe, pc):
            pe.wait_ge(x_copied, pc + 1)
            for t in range(CT):
                mm = nc.tensor.matmul(bank_turn[:, NE * t:NE * (t + 1)], x_t[:, P * t:P * (t + 1)], rw_sb[:, :],
                                      start=True, stop=True)
            mm.then_inc(routed, 1)

        def pe_turn_comb(pe, pc):
            pe.wait_ge(comb_step, 2 * pc + 2)
            pe.nop(nofuse=True)
            for t in range(CT):
                mm = nc.tensor.transpose(bank_turn.bitcast(BF16)[0:3 * NE, P * t:P * (t + 1)],
                                         combparts[:, t, :, :].rearrange("p c e -> p (c e)"), identb[:, :])
            mm.then_inc(comb_turned, 1)

        def pe_turn_sum(pe, c):
            pe.wait_ge(out_copied, c + 2)
            if not isinstance(c, int) or c < NCHUNK - 1:
                pe.wait_ge(comb_copied, c + 2)
            for t in range(CT):
                mm = nc.tensor.transpose(bank_turn[:, P * t:P * (t + 1)], out_t[:, P * t:P * (t + 1)], ident[:, :])
            mm.then_inc(out_turned, 1)

        def pe_down(pe, c, e, k):
            n = (c * NE + e) * IT + k
            pe.wait_ge(y_rounded, n + 1)
            if e == 0 and k == 0:
                pe.wait_ge(out_copied, c + 1)
            col = 2 * INTER + C * k
            for i, (w, yy) in enumerate(((w_hi, y_hi), (w_lo, y_hi), (w_hi, y_lo))):
                if i == 2:
                    pe.wait_ge(y_split, n + 5)
                mm = nc.tensor.matmul(bank_out, w[:, e, col:col + C], yy[:, e % 2, k, :],
                                      start=e + k + i == 0, stop=e == NE - 1 and k == IT - 1 and i == 2)
            mm.then_inc(down_done, 1)

        DOWN_LAG = 2 * IT - 1

        def pe_chunk(pe, c, first=False, last=False):
            tok = bass.ds(c * CHUNK, CHUNK)
            pe.wait_ge(x_split, c + 1)

            def up(e, k):
                n = (c * NE + e) * IT + k
                for bank, col, read, ready in ((bank_gate[k], P * k, gate_read, gate_ready),
                                               (bank_up[k], INTER + P * k, up_read, up_ready)):
                    if first and e == 0:
                        pe.wait_ge(maxed if read is gate_read else exped, NB * STEPS * GH)
                    pe.wait_ge(read, n + 1)
                    for i, (w, xx) in enumerate(((w_hi, x_hi), (w_hi, x_lo), (w_lo, x_hi))):
                        mm = nc.tensor.matmul(bank, w[:, e, col:col + P], xx[:, tok], start=i == 0, stop=i == 2)
                    mm.then_inc(ready, 1)

            for e in range(NE):
                for k in range(IT):
                    up(e, k)
                    if k == 0:
                        if first and e == 0:
                            pe.wait_ge(consts, 6)
                            pe.wait_ge(m_copied, NB * STEPS)
                        if first and e == 1:
                            pe.wait_ge(o_copied, NB * 4)
                        if e == 0:
                            pe.wait_ge(comb_copied, c + 1)
                        if not (first and e < 2):
                            pe.wait_ge(y_ready, (c * NE + e - 1) * IT)
                        pe.nop(nofuse=True)
                        nc.tensor.matmul(bank_comb[e % 2], pick[:, e, :], comb_t[:, tok], start=True, stop=True)\
                            .then_inc(comb_spread, 1)
                    if first and (e, k) == (0, 0):
                        pe_turn_out(pe, NB - 1, 3)
                    if first and (e, k) == (0, 1):
                        pe_turn_y(pe, NB - 1)
                    if first and (e, k) == (1, 0):
                        pe_project(pe, NB - 1)
                    if first and (e, k) == (1, 1):
                        pe.wait_ge(normed, 3 * (4 * NB - 1))
                    due = IT * e + k - DOWN_LAG
                    if due >= 0:
                        pe_down(pe, c, due // IT, due % IT)
                    elif not first:
                        pe_down(pe, c - 1, NE + due // IT, due % IT)
                    if (e, k) == (1, 1) and not first:
                        pe_turn_sum(pe, c - 1)
                    if not last:
                        if (e, k) == (3, 0):
                            pe_turn_x(pe, c + 1)
                        if (e, k) == (4, 0):
                            pe_route(pe, c + 1)
                        if (e, k) == (7, 1):
                            pe_turn_comb(pe, c + 1)

        def dve_norm_chunk(dve, pc, piece):
            if piece == 0:
                for t in range(CT):
                    nc.vector.bn_stats(stats2[:, t, :], x_all[:, CT * pc + t, :]).then_inc(norm_step, 1)
            elif piece == 1:
                dve.wait_ge(norm_step, NORM * pc + CT)
                dve.nop(nofuse=True)
                for t in range(CT):
                    nc.vector.bn_aggr(meanvar2[:, t, :], stats2[:, t, :]).then_inc(norm_step, 1)
                dve.wait_ge(norm_step, NORM * pc + 2 * CT)
                nc.vector.tensor_scalar(vareps2[:, :], meanvar2[:, :, 1], EPS, None, ALU.add)\
                    .then_inc(norm_step, 1)
            else:
                if piece == 2:
                    dve.wait_ge(rooted2, pc + 1)
                    if not isinstance(pc, int) or pc > 0:
                        dve.wait_ge(x_turned, pc)
                for t in range(2 * piece - 4, 2 * piece - 2):
                    nc.vector.tensor_scalar(xn2[:, t, :], x_all[:, CT * pc + t, :], meanvar2[:, t, 0:1],
                                            rstd2[:, t:t + 1], ALU.subtract, ALU.mult).then_inc(norm_step, 1)

        def dve_copy_x(dve, pc):
            dve.wait_ge(x_rounded, pc + 1)
            if not isinstance(pc, int) or pc > 0:
                dve.wait_ge(routed, pc)
                dve.wait_ge(x_split, pc)
            nc.vector.tensor_copy(x_t[:, :], bank_turn).then_inc(x_copied, 1)

        def dve_route(dve, pc, piece):
            step = ROUTE * pc
            r = bank_turn[:, 0:CT * NE].rearrange("p (t e) -> p t e", e=NE)
            other = prob[:, :, :].unsqueeze(2).to_broadcast([P, CT, NE, NE])
            own = prob[:, :, :].unsqueeze(3).to_broadcast([P, CT, NE, NE])
            if piece == 0:
                dve.wait_ge(routed, pc + 1)
                nc.vector.tensor_reduce(top[:, :], r, AX_X, ALU.max).then_inc(route_step, 1)
                dve.wait_ge(route_step, step + 1)
                nc.vector.scalar_tensor_tensor(out=logit[:, :, :], in0=r, scalar=1.0,
                                               in1=top[:, :].unsqueeze(2).to_broadcast([P, CT, NE]),
                                               op0=ALU.subtract, op1=ALU.subtract).then_inc(shifted_logits, 1)
            elif piece == 1:
                dve.wait_ge(expo_done, 2 * pc + 2)
                if not (isinstance(pc, int) and pc == 0):
                    nc.vector.reciprocal(silu_pos[:, :, :], silu_pos[:, :, :]).then_inc(divided, 1)
                    dve.wait_ge(divided, 2 * pc - 1)
                    nc.vector.tensor_tensor(expo[:, :, :], silu_neg[:, :, :], silu_pos[:, :, :], ALU.mult)\
                        .then_inc(divided, 1)
                    dve.wait_ge(divided, 2 * pc)
                nc.vector.tensor_reduce(top[:, :], expo[:, :, :], AX_X, ALU.add).then_inc(route_step, 1)
                dve.wait_ge(route_step, step + 2)
                nc.vector.reciprocal(total[:, :], top[:, :]).then_inc(route_step, 1)
                dve.wait_ge(route_step, step + 3)
                nc.vector.tensor_tensor(prob[:, :, :], expo[:, :, :],
                                        total[:, :].unsqueeze(2).to_broadcast([P, CT, NE]), ALU.mult)\
                    .then_inc(route_step, 1)
            elif piece == 2:
                dve.wait_ge(route_step, step + 4)
                if isinstance(pc, int) and pc == 0:
                    dve.wait_ge(consts, 2)
                nc.vector.tensor_tensor(above[:, :, :, :], other, own, ALU.is_gt).then_inc(route_step, 1)
                nc.vector.tensor_tensor(ties[:, :, :, :], other, own, ALU.is_ge).then_inc(route_step, 1)
                dve.wait_ge(route_step, step + 6)
                nc.vector.tensor_tensor(ties[:, :, :, :], ties[:, :, :, :],
                                        earlier[:, :, :].unsqueeze(1).to_broadcast([P, CT, NE, NE]), ALU.mult)\
                    .then_inc(route_step, 1)
            elif piece == 3:
                dve.wait_ge(route_step, step + 7)
                nc.vector.tensor_tensor(above[:, :, :, :], above[:, :, :, :], ties[:, :, :, :], ALU.max)\
                    .then_inc(route_step, 1)
                dve.wait_ge(route_step, step + 8)
                nc.vector.tensor_reduce(rank[:, :, :], above[:, :, :, :], AX_X, ALU.add).then_inc(route_step, 1)
                dve.wait_ge(route_step, step + 9)
                nc.vector.scalar_tensor_tensor(out=comb[:, :, :], in0=rank[:, :, :], scalar=float(TOPK),
                                               in1=prob[:, :, :], op0=ALU.is_lt, op1=ALU.mult)\
                    .then_inc(route_step, 1)
            elif piece == 4:
                dve.wait_ge(route_step, step + 10)
                if not isinstance(pc, int) or pc > 0:
                    dve.wait_ge(comb_turned, pc)
                nc.vector.tensor_copy(combparts[:, :, 0, :], comb[:, :, :]).then_inc(route_step, 1)
                dve.wait_ge(route_step, step + 11)
                nc.vector.tensor_tensor(combres[:, :, :], comb[:, :, :], combparts[:, :, 0, :], ALU.subtract)\
                    .then_inc(route_step, 1)
                dve.wait_ge(route_step, step + 12)
                nc.vector.tensor_copy(combparts[:, :, 1, :], combres[:, :, :]).then_inc(comb_step, 1)
                dve.wait_ge(comb_step, 2 * pc + 1)
                nc.vector.tensor_tensor(combparts[:, :, 2, :], combres[:, :, :], combparts[:, :, 1, :],
                                        ALU.subtract).then_inc(comb_step, 1)
            else:
                dve.wait_ge(comb_turned, pc + 1)
                nc.vector.tensor_copy(comb_t[:, bass.ds(pc * CHUNK, CHUNK)],
                                      bank_turn.bitcast(BF16)[0:3 * NE, 0:CHUNK]).then_inc(comb_copied, 1)

        def dve_add_sum(dve, c):
            dve.wait_ge(out_turned, c + 2)
            for t in range(CT):
                op = nc.vector.scalar_tensor_tensor(out=x_all[:, CT * c + t, :],
                                                    in0=bank_turn[:, P * t:P * (t + 1)],
                                                    scalar=tgate[:, 1:2], in1=x_all[:, CT * c + t, :],
                                                    op0=ALU.mult, op1=ALU.add)
            op.then_inc(out_added, 1)

        PREPARE = {(0, 0): (dve_norm_chunk, 0), (0, 1): (dve_norm_chunk, 1), (1, 1): (dve_norm_chunk, 2), (2, 1): (dve_norm_chunk, 3), (3, 1): (dve_copy_x,), (4, 1): (dve_route, 0), (5, 0): (dve_route, 1), (5, 1): (dve_route, 2), (6, 0): (dve_route, 3), (6, 1): (dve_route, 4), (7, 1): (dve_route, 5)}

        def dve_chunk(dve, c, first=False, last=False):
            for e in range(NE):
                for k in range(IT):
                    n = (c * NE + e) * IT + k
                    if first and (e, k) == (1, 0):
                        dve_residual(dve, NB - 1)
                    dve.wait_ge(up_ready, n + 1)
                    dve.wait_ge(gate_read, n + 3)
                    nc.vector.tensor_tensor(gated[:, k, :], silu[:, k, :], bank_up[k], ALU.mult)\
                        .then_inc(up_read, 1)
                    dve.wait_ge(up_read, n + 3)
                    dve.wait_ge(comb_spread, c * NE + e + 1)
                    dve.wait_ge(y_split, n + 1)
                    nc.vector.tensor_tensor(y[:, e % 2, k, :], gated[:, k, :], bank_comb[e % 2], ALU.mult)\
                        .then_inc(y_ready, 1)
                    if (e, k) == (2, 0) and not first:
                        dve_add_sum(dve, c - 1)
                    if not last and (e, k) in PREPARE:
                        step, *piece = PREPARE[e, k]
                        step(dve, c + 1, *piece)

        def act_round_x(act, pc):
            act.wait_ge(x_turned, pc + 1)
            nc.scalar.copy(x_hi[:, bass.ds(pc * CHUNK, CHUNK)], bank_turn).then_inc(x_rounded, 1)

        def act_exp_logits(act, pc):
            act.wait_ge(shifted_logits, pc + 1)
            if isinstance(pc, int) and pc == 0:
                nc.scalar.activation(expo[:, :, :], logit[:, :, :], ACT.Exp).then_inc(expo_done, 2)
            else:
                nc.scalar.activation(silu_neg[:, :, :], logit[:, :, :], ACT.Silu).then_inc(expo_done, 1)
                nc.scalar.activation(silu_pos[:, :, :], logit[:, :, :], ACT.Silu, scale=-1.0).then_inc(expo_done, 1)

        def act_copy_sum(act, c):
            act.wait_ge(down_done, 4 + NE * IT * (c + 1))
            act.wait_ge(out_turned, c + 1)
            nc.scalar.copy(out_t[:, :], bank_out).then_inc(out_copied, 1)

        def act_chunk(act, c, first=False, last=False):
            def round_y(e, k):
                n = (c * NE + e) * IT + k
                act.wait_ge(y_ready, n + 1)
                act.wait_ge(down_done, n + 1)
                nc.scalar.copy(y_hi[:, e % 2, k, :], y[:, e % 2, k, :]).then_inc(y_rounded, 1)

            for e in range(NE):
                for k in range(IT):
                    n = (c * NE + e) * IT + k
                    act.wait_ge(gate_ready, n + 1)
                    act.wait_ge(up_read, n + 1)
                    nc.scalar.activation(silu[:, k, :], bank_gate[k], ACT.Silu).then_inc(gate_read, 1)
                    if first and (e, k) == (0, 1):
                        act_copy_y(act, NB - 1)
                    if k == 1:
                        round_y(e, 0)
                    elif e > 0:
                        round_y(e - 1, 1)
                    if (e, k) == (1, 0) and not first:
                        act_copy_sum(act, c - 1)
                    if not last and (e, k) == (3, 1):
                        act_round_x(act, c + 1)
                    if not last and (e, k) == (5, 0):
                        act_exp_logits(act, c + 1)
            round_y(NE - 1, 1)

        def pool_root_experts(pool, pc):
            pool.wait_ge(norm_step, NORM * pc + 2 * CT + 1)
            nc.gpsimd.tensor_tensor(rstd2[:, :], vareps2[:, :], minus_half[:, :], ALU.pow).then_inc(rooted2, 1)

        def pool_split_x(pool, pc):
            pool.wait_ge(x_rounded, pc + 1)
            pool.wait_ge(x_copied, pc + 1)
            nc.gpsimd.tensor_tensor(x_lo[:, bass.ds(pc * CHUNK, CHUNK)], x_t[:, :],
                                    x_hi[:, bass.ds(pc * CHUNK, CHUNK)].bitcast(F32), ALU.subtract)\
                .then_inc(x_split, 1)

        def pool_chunk(pool, c, first=False, last=False):
            for e in range(NE):
                for k in range(IT):
                    n = (c * NE + e) * IT + k
                    pool.wait_ge(y_rounded, n + 1)
                    pool.wait_ge(down_done, n + 1)
                    nc.gpsimd.tensor_tensor(y_lo[:, e % 2, k, :], y[:, e % 2, k, :],
                                            y_hi[:, e % 2, k, :].bitcast(F32), ALU.subtract).then_inc(y_split, 1)
                    if not last and (e, k) == (0, 1):
                        pool_root_experts(pool, c + 1)
                    if not last and (e, k) == (4, 0):
                        pool_split_x(pool, c + 1)

        def chunks(eng, run):
            run(eng, 0, first=True)
            with eng.Fori(1, NCHUNK - 1) as c:
                run(eng, c)
            run(eng, NCHUNK - 1, last=True)

        def pe_scores(pe, b, par, s):
            attn, h0 = group(s)
            for j in range(GH):
                if s == attn and j == 0:
                    pe.wait_ge(stacked[QC if attn else Q], 16 * NP * (b + 1))
                    pe.wait_ge(stacked[KC if attn else K], 16 * (b + 1))
                yield
                u = (b * STEPS + s) * GH + j
                if not (isinstance(u, int) and u < 2):
                    pe.wait_ge(maxed, u - 1)
                q = qstack[par][0:ROWS, attn, h0 + j, :]
                k = kstack[par][0:ROWS, attn, h0 + j, :]
                a = bank_a[j % 2]
                if attn == 0:
                    nc.tensor.matmul(a[:, 0:P], q[:, 0:P], k[:, 0:P], start=True, stop=False)
                    nc.tensor.matmul(a[:, 0:P], identb[:, :], mask_qk[:, :], start=False, stop=True)
                    nc.tensor.matmul(a[:, P:P + T], q[:, P:T], k[:, :], start=True, stop=True)
                    mm = nc.tensor.matmul(a[:, T:T + P], identb[:, :], mask_qk[:, :], start=False, stop=True,
                                          skip_group_check=True)
                else:
                    nc.tensor.matmul(a[:, 0:T], q[:, 0:P], k[:, :], start=True, stop=True)
                    mm = nc.tensor.matmul(a[:, T:2 * T], q[:, P:T], k[:, :], start=True, stop=True)
                mm.then_inc(scored, 1)
                yield

        def pe_shifted(pe, b, par, s):
            attn, h0 = group(s)
            for j in range(GH):
                if j == 0:
                    pe.wait_ge(m_placed[s % 2], 16 * (b * 4 + s // 2 + 1))
                u = (b * STEPS + s) * GH + j
                if not (isinstance(u, int) and u < 2):
                    pe.wait_ge(exped, u - 1)
                q = qstack[par][0:MROWS, attn, h0 + j, :]
                k = kstack[par][0:MROWS, attn, h0 + j, :]
                s_b = bank_b[j % 2]
                if attn == 0:
                    nc.tensor.matmul(s_b[:, 0:T], k[:, 0:P], q[:, :], start=True, stop=True)
                    mm = nc.tensor.matmul(s_b[:, T:T + P], k[:, P:T], q[:, P:T], start=True, stop=True)
                else:
                    nc.tensor.matmul(s_b[:, 0:T], k[:, 0:P], q[:, :], start=True, stop=True)
                    mm = nc.tensor.matmul(s_b[:, T:2 * T], k[:, P:T], q[:, :], start=True, stop=True)
                mm.then_inc(shifted, 1)
                yield

        def pe_weigh(pe, b, par, s):
            attn, h0 = group(s)
            g = b * STEPS + s
            if attn == 0:
                pe.wait_ge(cleared, GH * (b * 4 + s // 2 + 1))
            else:
                pe.wait_ge(exped, GH * (g + 1))
            if s == 0:
                pe.wait_ge(front_dve, 6 * (b + 1))
            if attn == 0 and not (isinstance(g, int) and g == 0):
                pe.wait_ge(o_copied, b * 4 + s // 2)
            for key_tile in range(QT):
                for j in range(GH):
                    first = key_tile == 0
                    skip = P if attn == 0 and not first else 0
                    pr = probs[:, GH * (s % 2) + j, T * key_tile:T * (key_tile + 1) - skip]
                    mm = nc.tensor.matmul(bank_o[QUAD * j:QUAD * (j + 1), T * attn + skip:T * (attn + 1)],
                                          vext[:, par, attn, key_tile, h0 + j, :], pr, start=first,
                                          stop=True, skip_group_check=True)
                if not first:
                    mm.then_inc(weighed, 1)
                yield

        def pe_turn_max(pe, b, s):
            g = b * STEPS + s
            pe.wait_ge(msplit, 5 * (g + 1))
            if not (isinstance(g, int) and g == 0):
                pe.wait_ge(m_copied, g)
            for t in range(QT):
                mm = nc.tensor.transpose(bank_m[0:3 * GH, P * t:P * (t + 1)],
                                         mparts[:, s % 2, t, :, :].rearrange("p c h -> p (c h)"), identb[:, :])
            mm.then_inc(m_turned, 1)

        def pe_turn_out(pe, b, r):
            pair = b * 4 + r
            pe.wait_ge(o_copied, pair + 1)
            if r == 0 and not (isinstance(b, int) and b == 0):
                pe.wait_ge(x1_step, 2 * b)
            if r > 0:
                pe.wait_ge(normed, 3 * pair)
            for n in range(4):
                mm = nc.tensor.transpose(tail_bank(b, r)[:, P * n:P * (n + 1)], o_sb[:, r % 2, P * n:P * (n + 1)],
                                         ident[:, :])
            mm.then_inc(o_turned, 1)

        def pe_turn_y(pe, b):
            pe.wait_ge(normed, 3 * 4 * (b + 1))
            for t in range(QT):
                mm = nc.tensor.transpose(tail_bank(b)[:, P * t:P * (t + 1)], y_sb[:, t, :], ident[:, :])
            mm.then_inc(y_turned, 1)

        def pe_project(pe, b):
            pe.wait_ge(y_copied, b + 1)
            for t in range(QT):
                mm = nc.tensor.matmul(tail_bank(b)[:, P * t:P * (t + 1)], yT[:, P * t:P * (t + 1)], wp_sb[:, :],
                                      start=True, stop=True)
            mm.then_inc(projected, 1)

        def pe_front(pe, b, par, item):
            startup = isinstance(b, int) and b == 0
            bank = front_bank(b, item)
            if item == 0:
                if not startup:
                    pe.wait_ge(front_dve, 6 * b)
                pe.wait_ge(x_normed, 2 * (b + 1))
                for t in range(QT):
                    mm = nc.tensor.transpose(bank[:, P * t:P * (t + 1)], xn[:, t, :], ident[:, :])
            elif item <= 4:
                n = item - 1
                if n == 0:
                    pe.wait_ge(front_act, 5 * b + 1)
                elif not startup:
                    pe.wait_ge(front_dve, 6 * b + n)
                if n == KC:
                    pe.wait_ge(ctx_loaded[par], 8 * (b - par) + 16)
                    pe.nop(nofuse=True)
                w, src = (wck_sb, ctxT[:, par, :]) if n == KC else (wqk_sb[:, n, :], xnT)
                mm = nc.tensor.matmul(bank[:, 0:T], w[:, :], src[:, :], start=True, stop=True)
            else:
                if not startup:
                    pe.wait_ge(front_dve, 6 * b + item - 1)
                src, w = (xnT, wv_sb) if item == 5 else (ctxT[:, par, :], wcv_sb)
                for t in range(QT):
                    mm = nc.tensor.matmul(bank[:, P * t:P * (t + 1)], src[:, P * t:P * (t + 1)], w[:, :],
                                          start=True, stop=True)
            mm.then_inc(front_filled, 1)

        def later(b, par, s, by):
            return (b, par, s + by) if s + by < STEPS else (b + 1, 1 - par, s + by - STEPS)

        def pe_batch(pe, b, par, first=False, last=False):
            for s in range(STEPS):
                ahead = None if last and s + LEAD >= STEPS else pe_scores(pe, *later(b, par, s, LEAD))
                shift = pe_shifted(pe, b, par, s)
                weigh = None
                if s > 0:
                    weigh = pe_weigh(pe, b, par, s - 1)
                elif not first:
                    weigh = pe_weigh(pe, b - 1, 1 - par, STEPS - 1)
                for j in range(GH):
                    next(shift)
                    if ahead:
                        next(ahead)
                        next(ahead)
                    if j == 0 and s == 2 and not first:
                        pe_project(pe, b - 1)
                    if weigh and (j in (1, 2) if s % 2 else j in (0, 1)):
                        next(weigh)
                    if not last and (s, j) in FRONT_SLOTS:
                        pe_front(pe, b + 1, 1 - par, FRONT_SLOTS.index((s, j)))
                    if j == 3:
                        if not (last and s + TURN >= STEPS):
                            tb, _, ts = later(b, par, s, TURN)
                            pe_turn_max(pe, tb, ts)
                        if s == 1 and not first:
                            pe_turn_y(pe, b - 1)
                        if s % 2 == 0 and s > 0:
                            pe_turn_out(pe, b, s // 2 - 1)
                        elif s == 0 and not first:
                            pe_turn_out(pe, b - 1, 3)
                    if last and (s, j) == (4, 1):
                        pe.wait_ge(front_dve, 6 * NB)
                        pe_turn_x(pe, 0)
                    if last and (s, j) == (5, 1):
                        pe_route(pe, 0)
                    if last and (s, j) == (7, 1):
                        pe_turn_comb(pe, 0)

        def dve_statistics(dve, b):
            for t in range(QT):
                nc.vector.bn_stats(stats[:, t, :], x_all[:, QT * b + t, :]).then_inc(ln_step, 1)
            for t in range(QT):
                dve.wait_ge(ln_step, 5 * b + 1 + t)
                dve.nop(nofuse=True)
                nc.vector.bn_aggr(meanvar[:, t, :], stats[:, t, :]).then_inc(ln_step, 1)
            dve.wait_ge(ln_step, 5 * b + 4)
            nc.vector.tensor_scalar(vareps[:, :], meanvar[:, :, 1], EPS, None, ALU.add).then_inc(ln_step, 1)

        def dve_norm_x(dve, b):
            dve.wait_ge(rooted, b + 1)
            if not (isinstance(b, int) and b == 0):
                dve.wait_ge(front_filled, 7 * (b - 1) + 1)
            for t in range(QT):
                nc.vector.tensor_scalar(xn[:, t, :], x_all[:, QT * b + t, :], meanvar[:, t, 0:1], rstd[:, t:t + 1],
                                        ALU.subtract, ALU.mult).then_inc(x_normed, 1)

        def dve_max(dve, b, s):
            attn, _ = group(s)
            for j in range(GH):
                g = b * STEPS + s
                dve.wait_ge(scored, GH * g + j + 1)
                if j == 0 and not (isinstance(g, int) and g < 4):
                    dve.wait_ge(msplit, 5 * (g - 3))
                a = bank_a[j % 2]
                if attn == 0:
                    nc.vector.tensor_reduce(rowmax[:, s % 4, 0, j:j + 1], a[:, 0:P], AX_X, ALU.max)
                    op = nc.vector.tensor_reduce(rowmax[:, s % 4, 1, j:j + 1], a[:, P:P + T], AX_X, ALU.max)
                else:
                    op = nc.vector.tensor_reduce(rowmax[:, s % 4, :, j], a.rearrange("p (t k) -> p t k", t=QT),
                                                 AX_X, ALU.max)
                op.then_inc(maxed, 1)
                yield

        def dve_front(dve, b, par, item):
            if 1 <= item <= 4:
                n = item - 1
                dve.wait_ge(front_act, 5 * b + 2 + n)
                nc.vector.scalar_tensor_tensor(out=resid[:, n, :], in0=front_bank(b, item)[:, 0:T], scalar=bqk_sb[:, n:n + 1],
                                               in1=part[:, n, 0, :], op0=ALU.add, op1=ALU.subtract)\
                    .then_inc(front_dve, 1)
            elif item in (5, 6):
                dve.wait_ge(front_filled, 7 * b + item + 1)
                if not isinstance(b, int) or b > 1:
                    dve.wait_ge(weighed, STEPS * (b - 1))
                attn = item - 5
                nc.vector.tensor_tensor(
                    vext[:, par, attn, :, :, 0:D],
                    front_bank(b, item)[:, 0:T].rearrange("p (t h d) -> p t h d", t=QT, d=D),
                    bvp_sb[:, attn, :].rearrange("p (h d) -> p h d", d=D).unsqueeze(1).to_broadcast([P, QT, H, D]),
                    ALU.add).then_inc(front_dve, 1)

        def dve_norm_out(dve, b, r):
            pair = b * 4 + r
            dve.wait_ge(o_turned, pair + 1)
            t = tail_bank(b, r).rearrange("p (a t j f) -> p a t j f", a=2, t=QT, j=GH)
            nc.vector.reciprocal(rden[:, :, :, :], t[:, :, :, :, D]).then_inc(normed, 1)
            dve.wait_ge(normed, 3 * pair + 1)
            at = "p a t j f -> p (a t) j f"
            nc.vector.tensor_tensor(ynorm[:, :, :, :, :].rearrange(at), t.rearrange(at)[:, :, :, 0:D],
                                    rden[:, :, :, :].rearrange("p a t j -> p (a t) j").unsqueeze(3)
                                    .to_broadcast([P, 2 * QT, GH, D]), ALU.mult).then_inc(normed, 1)
            dve.wait_ge(normed, 3 * pair + 2)
            if r == 0 and not (isinstance(b, int) and b == 0):
                dve.wait_ge(y_turned, b)
            nc.vector.tensor_tensor(y_sb[:, :, QUAD * r:QUAD * (r + 1)].rearrange("p t (j d) -> p t j d", d=D),
                                    ynorm[:, 0], ynorm[:, 1], ALU.add).then_inc(normed, 1)

        def dve_residual(dve, b):
            dve.wait_ge(projected, b + 1)
            nc.vector.tensor_tensor(proj_b[:, :, :], tail_bank(b)[:, 0:T].rearrange("p (t c) -> p t c", t=QT),
                                    bvp_sb[:, 2, :].unsqueeze(1).to_broadcast([P, QT, C]), ALU.add)\
                .then_inc(x1_step, 1)
            dve.wait_ge(x1_step, 2 * b + 1)
            for t in range(QT):
                op = nc.vector.scalar_tensor_tensor(out=x_all[:, QT * b + t, :], in0=proj_b[:, t, :],
                                                    scalar=tgate[:, 0:1], in1=x_all[:, QT * b + t, :],
                                                    op0=ALU.mult, op1=ALU.add)
            op.then_inc(x1_step, 1)

        PREPARE_FIRST = {(1, 1): (dve_norm_chunk, 0), (1, 3): (dve_norm_chunk, 1), (3, 1): (dve_norm_chunk, 2),
                         (3, 3): (dve_norm_chunk, 3), (4, 3): (dve_copy_x,), (5, 1): (dve_route, 0),
                         (5, 3): (dve_route, 1), (6, 0): (dve_route, 2), (6, 1): (dve_route, 3),
                         (6, 3): (dve_route, 4), (7, 1): (dve_route, 5)}

        def dve_batch(dve, b, par, first=False, last=False):
            for s in range(STEPS):
                ahead = None
                if not (last and s + LEAD >= STEPS):
                    ab, _, a_s = later(b, par, s, LEAD)
                    ahead = dve_max(dve, ab, a_s)
                for j in range(GH):
                    if ahead:
                        next(ahead)
                    if not last and (s, j) == (0, 0):
                        dve_statistics(dve, b + 1)
                    if not last and (s, j) == (0, 2):
                        dve_norm_x(dve, b + 1)
                    if not last and (s, j) in FRONT_SLOTS:
                        dve_front(dve, b + 1, 1 - par, FRONT_SLOTS.index((s, j)))
                    if (s, j) == (2, 0) and not first:
                        dve_residual(dve, b - 1)
                    if j == 3:
                        if s % 2 == 0 and s > 0:
                            dve_norm_out(dve, b, s // 2 - 1)
                        elif s == 0 and not first:
                            dve_norm_out(dve, b - 1, 3)
                    if last and (s, j) in PREPARE_FIRST:
                        step, *piece = PREPARE_FIRST[s, j]
                        if step is dve_norm_chunk and piece == [0]:
                            dve.wait_ge(shifted, (NB - 1) * STEPS * GH)
                        step(dve, 0, *piece)

        def act_exp(act, b, s):
            attn, _ = group(s)
            width = P + T if attn == 0 else 2 * T
            g = b * STEPS + s
            for j in range(GH):
                act.wait_ge(shifted, GH * g + j + 1)
                if j == 0 and not (isinstance(g, int) and g < 2):
                    act.wait_ge(weighed, g - 1)
                nc.scalar.activation(probs[:, GH * (s % 2) + j, 0:width], bank_b[j % 2][:, 0:width], ACT.Exp,
                                     scale=SCALE).then_inc(exped, 1)
                yield

        def act_front(act, b, item):
            if item > 4:
                return
            act.wait_ge(front_filled, 7 * b + item + 1)
            if item == 0:
                nc.scalar.copy(xnT[:, :], front_bank(b, item)[:, 0:T]).then_inc(front_act, 1)
            else:
                n = item - 1
                if not isinstance(b, int) or b > 0:
                    act.wait_ge(parts_out[n], 16 * b)
                nc.scalar.activation(part[:, n, 0, :], front_bank(b, item)[:, 0:T], ACT.Identity, bias=bqk_sb[:, n:n + 1])\
                    .then_inc(front_act, 1)

        def act_front_mid(act, b, n):
            act.wait_ge(front_dve, 6 * b + n + 1)
            nc.scalar.copy(part[:, n, 1, :], resid[:, n, :]).then_inc(front_mid, 1)

        def act_copy_max(act, b, s):
            g = b * STEPS + s
            act.wait_ge(m_turned, g + 1)
            if not (isinstance(g, int) and g < 2):
                act.wait_ge(m_placed[s % 2], 16 * (b * 4 + s // 2))
            nc.scalar.copy(mrows[:, s % 2, :], bank_m[0:3 * GH, 0:T]).then_inc(m_copied, 1)

        def act_place_max(act, b, par, s):
            attn, h0 = group(s)
            act.wait_ge(m_copied, b * STEPS + s + 1)
            act.dma_start(qstack[par][ROWS:MROWS, attn, h0:h0 + GH, :], mrows[:, s % 2, :])\
                .then_inc(m_placed[s % 2], 16)

        def act_copy_out(act, b, r):
            act.wait_ge(weighed, b * STEPS + 2 * r + 2)
            if not (isinstance(b, int) and b == 0 and r < 2):
                act.wait_ge(o_turned, b * 4 + r - 1)
            nc.scalar.copy(o_sb[:, r % 2, :], bank_o).then_inc(o_copied, 1)

        def act_copy_y(act, b):
            act.wait_ge(y_turned, b + 1)
            nc.scalar.copy(yT[:, :], tail_bank(b)[:, 0:T]).then_inc(y_copied, 1)

        def act_weights_high(act, e):
            act.wait_ge(w_staged, 16 * (e + 1))
            nc.scalar.copy(w_hi[:, e, :], w_stage[:, :]).then_inc(w_hi_done, 1)

        PLACE_AT = 0
        MID_SLOTS = [(s + (j + 1) // GH, (j + 1) % GH) for s, j in FRONT_SLOTS[1:5]]

        def act_batch(act, b, par, first=False, last=False):
            for s in range(STEPS):
                e = act_exp(act, b, s)
                for j in range(GH):
                    next(e)
                    if j == PLACE_AT and s > 0 and not (last and s - 1 + TURN >= STEPS):
                        act_place_max(act, *later(b, par, s - 1, TURN))
                    elif j == PLACE_AT and s == 0 and not first:
                        act_place_max(act, b, par, TURN - 1)
                    if j == 1:
                        if s % 2 == 0 and s > 0:
                            act_copy_out(act, b, s // 2 - 1)
                        elif s == 0 and not first:
                            act_copy_out(act, b - 1, 3)
                    if j == 3:
                        if not (last and s + TURN >= STEPS):
                            tb, _, ts = later(b, par, s, TURN)
                            act_copy_max(act, tb, ts)
                        if s == 1 and not first:
                            act_copy_y(act, b - 1)
                    if (s, j) == (4, 3):
                        act_weights_high(act, b)
                    if last and (s, j) == (4, 2):
                        act_round_x(act, 0)
                    if last and (s, j) == (5, 2):
                        act_exp_logits(act, 0)
                    if not last and (s, j) in FRONT_SLOTS:
                        act_front(act, b + 1, FRONT_SLOTS.index((s, j)))
                    if not last and (s, j) in MID_SLOTS:
                        act_front_mid(act, b + 1, MID_SLOTS.index((s, j)))

        def pool_split_max(pool, b, s):
            g = b * STEPS + s
            n = 5 * g
            mp = mparts[:, s % 2]
            pool.wait_ge(maxed, GH * (g + 1))
            pool.nop(nofuse=True)
            nc.gpsimd.tensor_scalar(negmax[:, :, :], rowmax[:, s % 4], -1.0, None, ALU.mult).then_inc(msplit, 1)
            pool.wait_ge(msplit, n + 1)
            if not (isinstance(g, int) and g < 2):
                pool.wait_ge(m_turned, g - 1)
            pool.nop(nofuse=True)
            nc.gpsimd.tensor_copy(mp[:, :, 0, :], negmax[:, :, :]).then_inc(msplit, 1)
            pool.wait_ge(msplit, n + 2)
            nc.gpsimd.tensor_tensor(negres[:, :, :], negmax[:, :, :], mp[:, :, 0, :], ALU.subtract)\
                .then_inc(msplit, 1)
            pool.wait_ge(msplit, n + 3)
            pool.nop(nofuse=True)
            nc.gpsimd.tensor_copy(mp[:, :, 1, :], negres[:, :, :]).then_inc(msplit, 1)
            pool.wait_ge(msplit, n + 4)
            nc.gpsimd.tensor_tensor(mp[:, :, 2, :], negres[:, :, :], mp[:, :, 1, :], ALU.subtract)\
                .then_inc(msplit, 1)

        def pool_clear(pool, b, s, j):
            pool.wait_ge(exped, (b * STEPS + s) * GH + j + 1)
            pool.nop(nofuse=True)
            diagonal = probs[:, GH * (s % 2) + j, :].rearrange("p (a t) -> p a t", t=T)[:, :, 0:P]
            nc.gpsimd.affine_select(out=diagonal, in_=diagonal, compare_op=ALU.is_ge, fill=0.0, base=0,
                                    pattern=[[0, QT], [1, P]], channel_multiplier=-1).then_inc(cleared, 1)

        def pool_low(pool, b, n):
            pool.wait_ge(front_mid, 4 * b + n + 1)
            nc.gpsimd.tensor_tensor(part[:, n, 2, :], resid[:, n, :], part[:, n, 1, :], ALU.subtract)\
                .then_inc(low_done, 1)

        def pool_root(pool, b):
            pool.wait_ge(ln_step, 5 * b + 5)
            nc.gpsimd.tensor_tensor(rstd[:, :], vareps[:, :], minus_half[:, 0:QT], ALU.pow).then_inc(rooted, 1)

        def pool_weights_low(pool, e, half):
            pool.wait_ge(w_hi_done, e + 1)
            cols = slice(WCOLS // 2 * half, WCOLS // 2 * (half + 1))
            nc.gpsimd.tensor_tensor(w_lo[:, e, cols], w_stage[:, cols], w_hi[:, e, cols].bitcast(F32), ALU.subtract)\
                .then_inc(w_lo_done, 1)

        def pool_expert_constants(pool, n):
            if n == 0:
                pool.wait_ge(shifted, (NB - 1) * STEPS * GH)
                pool.nop(nofuse=True)
                nc.gpsimd.memset(earlier[:, :, :], 1.0).then_inc(consts, 1)
            elif n == 1:
                pool.wait_ge(consts, 1)
                nc.gpsimd.affine_select(out=earlier[:, :, :], in_=earlier[:, :, :], compare_op=ALU.is_ge, fill=0.0,
                                        base=-1, pattern=[[1, NE], [-1, NE]], channel_multiplier=0)\
                    .then_inc(consts, 1)
            elif n == 2:
                nc.gpsimd.memset(pick[:, :, :], 0.0).then_inc(consts, 1)
            elif n < 3 + NP:
                pool.wait_ge(consts, n)
                nc.gpsimd.affine_select(out=pick[:, :, :], in_=pick[:, :, :], compare_op=ALU.not_equal, fill=1.0,
                                        base=-NE * (n - 3), pattern=[[-1, NE], [0, P]], channel_multiplier=1)\
                    .then_inc(consts, 1)

        LOW_SLOTS = [(1, 0), (2, 1), (2, 3), (3, 0)]

        def pool_batch(pool, b, par, first=False, last=False):
            for s in range(STEPS):
                for j in range(GH):
                    if not last and (s, j) in LOW_SLOTS:
                        pool_low(pool, b + 1, LOW_SLOTS.index((s, j)))
                    if s % 2 == 0:
                        pool_clear(pool, b, s, j)
                    if not last and (s, j) == (0, 0):
                        pool_root(pool, b + 1)
                if not (last and s + LEAD >= STEPS):
                    ab, _, a_s = later(b, par, s, LEAD)
                    pool_split_max(pool, ab, a_s)
                if last:
                    pool_expert_constants(pool, s)
                    if s == 2:
                        pool_root_experts(pool, 0)
                    if s == 5:
                        pool_split_x(pool, 0)
                if s in (5, 6):
                    pool_weights_low(pool, b, s - 5)

        def sp_parts_out(sp, b, n):
            sp.wait_ge(low_done, 4 * b + n + 1)
            if not (isinstance(b, int) and b == 0):
                sp.nop(nofuse=True)
                sp.wait_ge(stacked[n], 16 * (NP if n in (Q, QC) else 1) * b)
            sp.dma_start(scratch[n].rearrange("a p t -> p a t"), part[:, n, :, :]).then_inc(parts_out[n], 16)

        def sp_stack(sp, b, par, n):
            attn = n // 2
            sp.wait_ge(parts_out[n], 16 * (b + 1))
            parts = scratch[n].rearrange("a (d h) t -> a d (h t)", d=D)
            if n in (K, KC):
                sp.dma_start(kstack[par][0:NP * PART_ROWS, attn, :, :].rearrange("p h t -> p (h t)"),
                             parts.unsqueeze(0).to_broadcast([NP, NP, D, H * T])).then_inc(stacked[n], 16)
            else:
                for a in range(NP):
                    rows = slice(PART_ROWS * a, PART_ROWS * (a + 1))
                    sp.dma_start(qstack[par][rows, attn, :, :].rearrange("p h t -> p (h t)"),
                                 parts[a].unsqueeze(0).to_broadcast([NP, D, H * T])).then_inc(stacked[n], 16)

        def sp_batch(sp, b, par, first=False, last=False):
            for s in range(STEPS):
                if s == 0 and not last:
                    if not first:
                        sp.wait_ge(front_filled, 7 * b)
                    sp.nop(nofuse=True)
                    sp.dma_start(ctxT[:, 1 - par, :], ctx_in[b + 1]).then_inc(ctx_loaded[1 - par], 16)
                if s == 2 and not last:
                    sp.wait_ge(shifted, b * STEPS * GH + 1)
                    sp.nop(nofuse=True)
                    sp_parts_out(sp, b + 1, K)
                    sp_stack(sp, b + 1, 1 - par, Q)
                if s == 3 and not last:
                    sp_stack(sp, b + 1, 1 - par, K)
                    sp_parts_out(sp, b + 1, KC)
                    sp_stack(sp, b + 1, 1 - par, QC)
                if s == 4 and not last:
                    sp_stack(sp, b + 1, 1 - par, KC)
                if s == 1:
                    if not first:
                        sp.wait_ge(w_lo_done, 2 * b)
                        sp.nop(nofuse=True)
                    sp.dma_start(w_stage[:, :], w12t[:, b, :]).then_inc(w_staged, 16)
                if s == 1 and not last:
                    sp_parts_out(sp, b + 1, Q)
                if s == 2 and not last:
                    sp_parts_out(sp, b + 1, QC)

        def words(stack, rows, par):
            return stack[par][rows].rearrange("p a h t -> p (a h t)").bitcast(mybir.dt.uint32)

        def stack_zeros(eng, stack, par):
            return eng.memset(words(stack, slice(64, ROWS), par), 0)

        def batches(eng, run):
            run(eng, 0, 0, first=True)
            with eng.Fori(0, NB // 2 - 1) as i:
                run(eng, 2 * i + 1, 1)
                run(eng, 2 * i + 2, 0)
            run(eng, NB - 1, 1, last=True)

        with nc.Block() as block:
            @block.sync
            def _(sp):
                sp.dma_start(x_all[:, 0:QT, :], x[:, 0:QT, :]).then_inc(x_in, 16)
                sp.dma_start(gate_sb[:, :], gates.unsqueeze(0).to_broadcast([P, 2])).then_inc(gate_in, 16)
                for dst, src in ((wqk_sb[:, :, :], wqk), (bqk_sb[:, :], bqk)):
                    sp.dma_start(dst, src).then_inc(qk_in, 16)
                sp.dma_start(ctxT[:, 0, :], ctx_in[0]).then_inc(ctx_loaded[0], 16)
                for dst, src in ((wck_sb[:, :], wck), (wv_sb[:, :], wv), (wcv_sb[:, :], wcv), (wp_sb[:, :], wp),
                                 (rw_sb[:, :], rwt), (bvp_sb[:, :, :], bvp.unsqueeze(0).to_broadcast([P, 3, C]))):
                    sp.dma_start(dst, src).then_inc(w_in, 16)
                sp.dma_start(x_all[:, QT:, :], x[:, QT:, :]).then_inc(rest_in, 16)
                for par in range(2):
                    sp.dma_start(words(kstack, slice(ROWS, MROWS), par), ones_in).then_inc(ones_placed, 16)
                sp.wait_ge(const_dve, 1)
                sp.wait_ge(const_pool, 8)
                for n in (Q, K):
                    sp_parts_out(sp, 0, n)
                sp_stack(sp, 0, 0, Q)
                sp_parts_out(sp, 0, QC)
                sp_stack(sp, 0, 0, K)
                sp_parts_out(sp, 0, KC)
                sp_stack(sp, 0, 0, QC)
                sp_stack(sp, 0, 0, KC)
                sp.wait_ge(const_pool, 10)
                batches(sp, sp_batch)
                with sp.Fori(0, NCHUNK) as c:
                    sp.wait_ge(out_added, c + 2)
                    sp.nop(nofuse=True)
                    sp.dma_start(out[:, bass.ds(c * CT, CT), :], x_all[:, bass.ds(c * CT, CT), :])\
                        .then_inc(stored, 16)
                sp.wait_ge(stored, 16 * NCHUNK)

            @block.gpsimd
            def _(pool):
                nc.gpsimd.memset(minus_half[:, :], -0.5).then_inc(const_pool, 1)
                nc.gpsimd.memset(ident[:, :], 0.0).then_inc(const_pool, 1)
                pool.wait_ge(const_pool, 2)
                nc.gpsimd.affine_select(out=ident[:, :], in_=ident[:, :], compare_op=ALU.not_equal, fill=1.0, base=0,
                                        pattern=[[-1, P]], channel_multiplier=1).then_inc(const_pool, 1)
                pool.wait_ge(const_pool, 3)
                for m in (identb, mask_qk):
                    nc.gpsimd.memset(m[:, :], 0.0).then_inc(const_pool, 1)
                pool.wait_ge(const_pool, 5)
                nc.gpsimd.affine_select(out=identb[:, :], in_=identb[:, :], compare_op=ALU.not_equal, fill=1.0,
                                        base=0, pattern=[[-1, P]], channel_multiplier=1).then_inc(const_pool, 1)
                nc.gpsimd.affine_select(out=mask_qk[:, :], in_=mask_qk[:, :], compare_op=ALU.is_ge, fill=MASKED,
                                        base=0, pattern=[[-1, P]], channel_multiplier=1).then_inc(const_pool, 1)
                pool_root(pool, 0)
                pool.wait_ge(rooted, 1)
                stack_zeros(nc.gpsimd, qstack, 0).then_inc(const_pool, 1)
                pool.wait_ge(const_pool, 8)
                for i in range(4):
                    pool_low(pool, 0, i)
                pool.wait_ge(low_done, 4)
                for stack in (qstack, kstack):
                    stack_zeros(nc.gpsimd, stack, 1).then_inc(const_pool, 1)
                pool.wait_ge(const_pool, 10)
                for s in range(LEAD):
                    pool_split_max(pool, 0, s)
                batches(pool, pool_batch)
                pool.nop().then_inc(y_split, 4)
                chunks(pool, pool_chunk)

            @block.scalar
            def _(act):
                act.wait_ge(gate_in, 16)
                nc.scalar.activation(tgate[:, :], gate_sb[:, :], ACT.Tanh).then_inc(gate_done, 1)
                act.wait_ge(qk_in, 32)
                for item in range(5):
                    act_front(act, 0, item)
                    if item > 1:
                        act_front_mid(act, 0, item - 2)
                act_front_mid(act, 0, KC)
                for s in range(TURN):
                    act_copy_max(act, 0, s)
                    act_place_max(act, 0, 0, s)
                batches(act, act_batch)
                act_copy_out(act, NB - 1, 3)
                act.nop().then_inc(gate_read, 2)
                act.nop().then_inc(out_copied, 1)
                chunks(act, act_chunk)
                act_copy_sum(act, NCHUNK - 1)

            @block.vector
            def _(dve):
                stack_zeros(nc.vector, kstack, 0).then_inc(const_dve, 1)
                dve.wait_ge(x_in, 16)
                dve_statistics(dve, 0)
                dve_norm_x(dve, 0)
                dve.wait_ge(qk_in, 32)
                for item in range(5):
                    dve_front(dve, 0, 0, item)
                dve.wait_ge(w_in, 16 * 6)
                for item in (5, 6):
                    dve_front(dve, 0, 0, item)
                nc.vector.memset(vext[:, :, :, :, :, D:D + 1], 1.0).then_inc(const_dve, 1)
                nc.vector.memset(vext[:, :, :, :, :, D + 1:], 0.0).then_inc(const_dve, 1)
                nc.vector.memset(vext[:, 1, :, :, :, 0:D], 0.0).then_inc(const_dve, 1)
                dve.wait_ge(rest_in, 16)
                dve.wait_ge(gate_done, 1)
                for s in range(LEAD):
                    for _step in dve_max(dve, 0, s):
                        pass
                batches(dve, dve_batch)
                dve.nop().then_inc(up_read, 2)
                dve.nop().then_inc(out_added, 1)
                dve_norm_out(dve, NB - 1, 3)
                chunks(dve, dve_chunk)
                dve_add_sum(dve, NCHUNK - 1)

            @block.tensor
            def _(pe):
                pe.wait_ge(const_pool, 3)
                pe_front(pe, 0, 0, 0)
                pe.wait_ge(qk_in, 32)
                for item in range(1, 4):
                    pe_front(pe, 0, 0, item)
                pe.wait_ge(w_in, 16 * 6)
                for item in range(4, 7):
                    pe_front(pe, 0, 0, item)
                pe.wait_ge(front_dve, 6)
                pe.wait_ge(const_pool, 7)
                for s in range(LEAD):
                    for n, _step in enumerate(pe_scores(pe, 0, 0, s)):
                        if n == GH and s > 0:
                            pe_turn_max(pe, 0, s - 1)
                pe.wait_ge(const_dve, 4)
                pe.wait_ge(ones_placed, 32)
                batches(pe, pe_batch)
                for _half in pe_weigh(pe, NB - 1, 1, STEPS - 1):
                    pass
                pe.nop().then_inc(down_done, 4)
                pe.nop().then_inc(out_turned, 1)
                chunks(pe, pe_chunk)
                for n in range(NE * IT - DOWN_LAG, NE * IT):
                    pe_down(pe, NCHUNK - 1, n // IT, n % IT)
                pe_turn_sum(pe, NCHUNK - 1)


def kernel(**inputs):
    import numpy as np
    from concourse import bacc
    from concourse.bass_utils import run_bass_kernel_spmd

    def a(name):
        return np.asarray(inputs[name])

    def turned(w):
        return np.ascontiguousarray(w.reshape(*w.shape[:-1], H, D).swapaxes(-1, -2).reshape(w.shape))

    x = "L0_xattn_"
    arrays = {
        "x": np.ascontiguousarray(a("x").reshape(NTILE, P, C).transpose(1, 0, 2)),
        "ctx_in": np.ascontiguousarray(a("ctx_512").transpose(0, 2, 1)),
        "gates": np.concatenate([a("g_xattn"), a("g_ffn")]),
        "wqk": np.ascontiguousarray(np.stack([turned(a(x + n)) for n in ("Wq", "Wk", "Wcq")], 1)),
        "wck": turned(a(x + "Wck")),
        "bqk": np.ascontiguousarray(np.stack([turned(a(x + n)) for n in ("bq", "bk", "bcq", "bck")], 1)),
        "wv": a(x + "Wv"), "wcv": a(x + "Wcv"), "wp": a(x + "Wp"),
        "bvp": np.stack([a(x + n) for n in ("bv", "bcv", "bp")]),
        "w12t": np.concatenate([
            a("L0_ffn_w1").transpose(2, 0, 1),
            a("L0_ffn_w2").reshape(NE, C, IT, P).transpose(3, 0, 2, 1).reshape(P, NE, IT * C)], 2),
        "ones_in": np.full((NP, H * T), BF16_ONES, np.uint32),
        "rwt": np.ascontiguousarray(a("L0_ffn_router_w").T),
    }
    nc = bacc.Bacc("TRN2", target_bir_lowering=False, num_devices=1)
    args = {n: nc.dram_tensor(n, v.shape, mybir.dt.from_np(v.dtype), kind="ExternalInput").ap()
            for n, v in arrays.items()}
    args["scratch"] = [nc.dram_tensor(f"parts{n}", (NP, P, T), BF16, kind="Internal").ap() for n in range(4)]
    args["out"] = nc.dram_tensor("out", (P, NTILE, C), F32, kind="ExternalOutput").ap()
    gated_attention_experts(nc, **args)
    r = run_bass_kernel_spmd(nc, [arrays], core_ids=[0])
    return r.results[0]["out"].transpose(1, 0, 2).reshape(NB, T, C)
```
